# Optimizing a Trainium2 kernel written in Bass

```python
import numpy as np
import jax
import jax.numpy as jnp

def _softmax(x, axis=-1):
    return jax.nn.softmax(x, axis=axis)

def _gelu(x):
    return jax.nn.gelu(x, approximate=True)

def _silu(x):
    return jax.nn.silu(x)

def _sigmoid(x):
    return jax.nn.sigmoid(x)

def _layernorm(x, axis=-1, eps=1e-05):
    m = jnp.mean(x, axis=axis, keepdims=True)
    v = jnp.var(x, axis=axis, keepdims=True)
    return (x - m) / jnp.sqrt(v + eps)

def _scatter_add(tgt, idx, src, axis=0):
    return tgt.at[idx].add(src)

def _segment_sum(src, seg, n):
    return jax.ops.segment_sum(src, seg, n)
kernel_name = 'mk_decoder_preln_d1_seqx_r8_ec0aa5'

def setup_inputs(seed: int=0):
    np.random.seed(seed)
    _w = jnp.asarray

    def _rec_inputs():
        import jax
        import jax.numpy as jnp
        _rk = jax.random.key(seed)
        x = -0.000125 + 0.9999 * jax.random.normal(jax.random.fold_in(_rk, 1), (2, 256, 256), jnp.float32)
        _lenS = 256 - jax.random.randint(jax.random.fold_in(_rk, 7), (2,), 0, max(1, 256 // 4) + 1, jnp.int32)
        _lenS2 = 512 - jax.random.randint(jax.random.fold_in(_rk, 8), (2,), 0, max(1, 512 // 4) + 1, jnp.int32)
        _ctx_2048P = jax.random.normal(jax.random.fold_in(_rk, 11), (2, 16, 256), jnp.float32)
        _ctx_2048c = jax.random.dirichlet(jax.random.fold_in(_rk, 511), 0.3 * jnp.ones((16,), jnp.float32), (2, 512))
        _ctx_2048t = jnp.einsum('bsk,bkd->bsd', _ctx_2048c, _ctx_2048P)
        _ctx_2048t = _ctx_2048t * jax.lax.rsqrt(jnp.mean(jnp.square(_ctx_2048t)) + 1e-12) * 0.953939
        ctx_2048 = -0.000514642 + 1.00011 * (_ctx_2048t + 0.3 * jax.random.normal(jax.random.fold_in(_rk, 611), (2, 512, 256), jnp.float32))
        _validS = jnp.arange(256)[None, :] < _lenS[:, None]
        _validS2 = jnp.arange(512)[None, :] < _lenS2[:, None]
        _causal = jnp.tril(jnp.ones((256, 256), dtype=bool))
        mask_BxS2_bk0 = jnp.logical_not(jnp.broadcast_to(_validS2[:, :], (2, 512)))
        return (x, ctx_2048, mask_BxS2_bk0)
    x, ctx_2048, mask_BxS2_bk0 = _rec_inputs()

    def _L0_attn_setup():
        import jax, jax.numpy as jnp
        import numpy as np
        N_HEADS = 16
        key = jax.random.key(seed)
        ks = jax.random.split(key, 9)
        B, S, D = (2, 256, 256)
        s = 0.02
        return {'X': jax.random.normal(ks[0], (B, S, D), jnp.float32), 'Wq': jax.random.normal(ks[1], (D, D), jnp.float32) * s, 'bq': jax.random.normal(ks[2], (D,), jnp.float32) * s, 'Wk': jax.random.normal(ks[3], (D, D), jnp.float32) * s, 'bk': jax.random.normal(ks[4], (D,), jnp.float32) * s, 'Wv': jax.random.normal(ks[5], (D, D), jnp.float32) * s, 'bv': jax.random.normal(ks[6], (D,), jnp.float32) * s, 'Wo': jax.random.normal(ks[7], (D, D), jnp.float32) * s, 'bo': jax.random.normal(ks[8], (D,), jnp.float32) * s}
    _L0_attn_all = _L0_attn_setup()
    _L0_attn_in = {k: v for k, v in _L0_attn_all.items() if k in ('Wq', 'bq', 'Wk', 'bk', 'Wv', 'bv', 'Wo', 'bo')}
    del _L0_attn_all

    def _L0_xattn_setup():
        import jax, jax.numpy as jnp
        import numpy as np
        key = jax.random.key(seed)
        k1, k2, k3 = jax.random.split(key, 3)
        B, S, D, M = (8, 256, 256, 128)
        hidden_states = jax.random.normal(k1, (B, S, D), dtype=jnp.float32)
        memory_tokens = jax.random.normal(k2, (B, M, D), dtype=jnp.float32)
        memory_mask = jax.random.randint(k3, (B, M), 0, 2).astype(jnp.bool_)
        return {'hidden_states': hidden_states, 'memory_tokens': memory_tokens, 'memory_mask': memory_mask}
    _L0_xattn_all = _L0_xattn_setup()
    _L0_xattn_in = {k: v for k, v in _L0_xattn_all.items() if k in ()}
    del _L0_xattn_all

    def _L0_ffn_setup():
        import jax, jax.numpy as jnp
        import numpy as np
        ALPHA = 1.702
        LIMIT = 7.0
        TOP_K = 4
        B, S, H = (1, 128, 256)
        E, D = (16, 256)
        key = jax.random.key(seed)
        ks = jax.random.split(key, 7)
        s = 0.02
        return {'hidden_states': jax.random.normal(ks[0], (B, S, H), dtype=jnp.float32), 'router_weight': jax.random.normal(ks[1], (E, H), dtype=jnp.float32) * s, 'router_bias': jax.random.normal(ks[2], (E,), dtype=jnp.float32) * s, 'gate_up_proj': jax.random.normal(ks[3], (E, H, 2 * D), dtype=jnp.float32) * s, 'gate_up_proj_bias': jax.random.normal(ks[4], (E, 2 * D), dtype=jnp.float32) * s, 'down_proj': jax.random.normal(ks[5], (E, D, H), dtype=jnp.float32) * s, 'down_proj_bias': jax.random.normal(ks[6], (E, H), dtype=jnp.float32) * s}
    _L0_ffn_all = _L0_ffn_setup()
    _L0_ffn_in = {k: v for k, v in _L0_ffn_all.items() if k in ('router_weight', 'router_bias', 'gate_up_proj', 'gate_up_proj_bias', 'down_proj', 'down_proj_bias')}
    del _L0_ffn_all
    return {'x': x, 'ctx_2048': ctx_2048, 'mask_BxS2_bk0': mask_BxS2_bk0, 'L0_attn_Wq': _L0_attn_in['Wq'], 'L0_attn_bq': _L0_attn_in['bq'], 'L0_attn_Wk': _L0_attn_in['Wk'], 'L0_attn_bk': _L0_attn_in['bk'], 'L0_attn_Wv': _L0_attn_in['Wv'], 'L0_attn_bv': _L0_attn_in['bv'], 'L0_attn_Wo': _L0_attn_in['Wo'], 'L0_attn_bo': _L0_attn_in['bo'], 'L0_ffn_router_weight': _L0_ffn_in['router_weight'], 'L0_ffn_router_bias': _L0_ffn_in['router_bias'], 'L0_ffn_gate_up_proj': _L0_ffn_in['gate_up_proj'], 'L0_ffn_gate_up_proj_bias': _L0_ffn_in['gate_up_proj_bias'], 'L0_ffn_down_proj': _L0_ffn_in['down_proj'], 'L0_ffn_down_proj_bias': _L0_ffn_in['down_proj_bias']}

def reference(x, ctx_2048, mask_BxS2_bk0, L0_attn_Wq, L0_attn_bq, L0_attn_Wk, L0_attn_bk, L0_attn_Wv, L0_attn_bv, L0_attn_Wo, L0_attn_bo, L0_ffn_router_weight, L0_ffn_router_bias, L0_ffn_gate_up_proj, L0_ffn_gate_up_proj_bias, L0_ffn_down_proj, L0_ffn_down_proj_bias):
    import jax
    import jax.numpy as jnp

    def _L0_attn_ref(X, Wq, bq, Wk, bk, Wv, bv, Wo, bo):
        import jax, jax.numpy as jnp
        import numpy as np
        N_HEADS = 16
        B, S, D = X.shape
        H = N_HEADS
        d_head = D // H
        scale = jnp.asarray(1.0 / np.sqrt(np.sqrt(d_head)), X.dtype)
        Q = (X @ Wq.T + bq).reshape(B, S, H, d_head) * scale
        K = (X @ Wk.T + bk).reshape(B, S, H, d_head) * scale
        V = (X @ Wv.T + bv).reshape(B, S, H, d_head)
        scores = jnp.einsum('bqhd,bkhd->bhqk', Q, K)
        causal = jnp.tril(jnp.ones((S, S), bool))
        scores = jnp.where(causal[None, None], scores, -jnp.inf)
        attn = jax.nn.softmax(scores.astype(jnp.float32), axis=-1).astype(X.dtype)
        out = jnp.einsum('bhqk,bkhd->bqhd', attn, V).reshape(B, S, D)
        return out @ Wo.T + bo

    def _L0_xattn_ref(hidden_states, memory_tokens, memory_mask):
        import jax, jax.numpy as jnp
        import numpy as np
        B, S, D = hidden_states.shape
        scale = 1.0 / jnp.sqrt(jnp.asarray(D, hidden_states.dtype))
        scores = jnp.einsum('bsd,bmd->bsm', hidden_states, memory_tokens) * scale
        neg_inf = jnp.asarray(-1e+30, scores.dtype)
        scores = jnp.where(memory_mask[:, None, :], scores, neg_inf)
        attn = jax.nn.softmax(scores, axis=-1)
        readout = jnp.einsum('bsm,bmd->bsd', attn, memory_tokens)
        valid_b = jnp.any(memory_mask, axis=-1)
        out = jnp.where(valid_b[:, None, None], readout, jnp.zeros_like(readout))
        return out

    def _L0_ffn_ref(hidden_states, router_weight, router_bias, gate_up_proj, gate_up_proj_bias, down_proj, down_proj_bias):
        import jax, jax.numpy as jnp
        import numpy as np
        ALPHA = 1.702
        LIMIT = 7.0
        TOP_K = 4
        B, S, H = (1, 128, 256)
        E, D = (16, 256)
        batch, seq, hdim = hidden_states.shape
        x = hidden_states.reshape(-1, hdim)
        T = x.shape[0]
        logits = x @ router_weight.T + router_bias
        top_val, top_idx = jax.lax.top_k(logits, TOP_K)
        top_val = jax.nn.softmax(top_val, axis=-1)
        router_scores = jnp.zeros_like(logits).at[jnp.arange(T)[:, None], top_idx].set(top_val)
        gate_up = jnp.einsum('th,ehd->etd', x, gate_up_proj) + gate_up_proj_bias[:, None, :]
        gate = gate_up[..., ::2]
        up = gate_up[..., 1::2]
        gate = jnp.minimum(gate, LIMIT)
        up = jnp.clip(up, -LIMIT, LIMIT)
        glu = gate * jax.nn.sigmoid(gate * ALPHA)
        out = jnp.einsum('etd,edh->eth', (up + 1.0) * glu, down_proj) + down_proj_bias[:, None, :]
        out = out * router_scores.T[:, :, None]
        out = out.sum(axis=0)
        return out.reshape(batch, seq, hdim)
    x = x + _L0_attn_ref(_layernorm(x, axis=-1), L0_attn_Wq, L0_attn_bq, L0_attn_Wk, L0_attn_bk, L0_attn_Wv, L0_attn_bv, L0_attn_Wo, L0_attn_bo)
    x = x + _L0_xattn_ref(_layernorm(x, axis=-1), ctx_2048, mask_BxS2_bk0)
    x = x + _L0_ffn_ref(_layernorm(x, axis=-1), L0_ffn_router_weight, L0_ffn_router_bias, L0_ffn_gate_up_proj, L0_ffn_gate_up_proj_bias, L0_ffn_down_proj, L0_ffn_down_proj_bias)
    return x

_drawn_inputs = setup_inputs


def setup_inputs(seed=0):
    import zlib

    import numpy as np

    out = dict(_drawn_inputs(seed))
    spreads = {}
    factors = {'L0_attn_Wq': 8.0,
     'L0_attn_bq': 8.0,
     'L0_attn_Wk': 8.0,
     'L0_attn_bk': 64.0,
     'L0_attn_Wv': 3.89,
     'L0_attn_bv': 8.0,
     'L0_attn_Wo': 3.657,
     'L0_attn_bo': 3.177,
     'L0_ffn_router_bias': 8.0,
     'L0_ffn_gate_up_proj_bias': 43.906,
     'L0_ffn_down_proj_bias': 6.436,
     'L0_ffn_gate_up_proj': 3.075,
     'L0_ffn_down_proj': 2.695}
    for name, (base, spread) in spreads.items():
        noise = np.random.default_rng([zlib.crc32(name.encode()), seed]).standard_normal(out[name].shape)
        drawn = base * np.exp(spread * noise) if base else spread * noise
        out[name] = jnp.asarray(drawn.astype(out[name].dtype))
    for name, factor in factors.items():
        out[name] = (out[name] * factor).astype(out[name].dtype)
    return out
```

```python
from contextlib import ExitStack

import concourse.bass as bass
from concourse import mybir

F32 = mybir.dt.float32
F32R = mybir.dt.float32r
BF16 = mybir.dt.bfloat16
U8 = mybir.dt.uint8
ALU = mybir.AluOpType
ACT = mybir.ActivationFunctionType
AX = mybir.AxisListType

P = 128
B, S, D = 2, 256, 256
M = 512
H, DH = 16, 16
E, F = 16, 256
TOP_K = 4
T = B * S
NC = T // P
QC = S // P
KD = D // P
KM = M // P
HG = 4
NG = H // HG
G8 = P // DH
HP = 32
EPS = 1e-5
ALPHA, LIMIT = 1.702, 7.0
NEG = -1e30
GU = 2 * F * KD
DW = D * KD


def decoder_layer(nc, x_d, ctx_d, ctxT_d, wqkv_d, wo_d, params_d, rows_d, mask_d, dbias_d, we_d, out_d):
    ctx = ExitStack()
    with ctx:
        def sb(name, shape, dt=F32):
            return ctx.enter_context(nc.sbuf_tensor(name, shape, dt))

        def sem(name):
            return ctx.enter_context(nc.semaphore(name))

        PS = ctx.enter_context(nc.psum_tensor("PS", [P, 8, 512], F32))

        x = sb("x", [P, NC, D])
        ctx_sb = sb("ctx_sb", [P, B * KM, D])
        ctxT = sb("ctxT", [P, B * KD, M])
        wqkv = sb("wqkv", [P, 3, KD, D])
        wo = sb("wo", [P, NG, D])
        params = sb("params", [P, 4 + 4 * E + KD * E])
        rows = sb("rows", [P, 2 * D + E])
        mask8 = sb("mask8", [1, B * M], U8)
        dbias = sb("dbias", [E, D])
        raw = [sb(f"raw{i}", [P, GU + DW]) for i in range(2)]
        bq, bk = params[:, 0:2], params[:, 2:4]
        gub = params[:, 4:4 + 4 * E].rearrange("p (e g m) -> p e g m", e=E, g=2)
        routerT = params[:, 4 + 4 * E:].rearrange("p (k e) -> p k e", k=KD)
        bv_b, bo_b, rb_b = rows[:, 0:D], rows[:, D:2 * D], rows[:, 2 * D:]

        ident = sb("ident", [P, P])
        ident_bf = sb("ident_bf", [P, P], BF16)
        causal = sb("causal", [P, P], BF16)
        headmask = sb("headmask", [P, G8])
        sumsel = sb("sumsel", [P, P])
        ones_bf = sb("ones_bf", [1, P], BF16)
        ones_f = sb("ones_f", [P, E])
        one1 = sb("one1", [1, P])
        eps_t = sb("eps_t", [P, 1])

        xb = sb("xb", [P, NC, D])
        xn = sb("xn", [P, NC, D])
        xT = sb("xT", [P, KD, T])
        qT = sb("qT", [P, KD, T])
        kT = sb("kT", [P, KD, T])
        kblk = sb("kblk", [P, B * KD, G8, S])
        vp = sb("vp", [P, NC, H, HP])
        pr0 = sb("pr0", [P, HG, P])
        pr1 = sb("pr1", [P, HG, S])
        pt0 = sb("pt0", [P, HG, P])
        pt1 = sb("pt1", [P, QC, HG, P])
        nmax = sb("nmax", [P, 2, HG])
        osum = sb("osum", [P, NG, T])
        rsum = sb("rsum", [P, 2, S])
        attT = sb("attT", [P, NG, T])
        x2 = sb("x2", [P, NC, D])
        x3 = sb("x3", [P, NC, D])
        stats = sb("stats", [P, NC, 6])
        mv = sb("mv", [P, NC, 2])
        ve = sb("ve", [P, NC])
        lnv = sb("lnv", [P, NC])
        rstd0 = sb("rstd0", [P, NC])
        nw = sb("nw", [P, 3, NC])
        rstd = sb("rstd", [P, NC])
        maskf = sb("maskf", [1, B * M])
        pen = sb("pen", [1, B * M], BF16)
        valid1 = sb("valid1", [1, B])
        valid = sb("valid", [P, B])
        xmax = sb("xmax", [P, NC])
        xbias = sb("xbias", [P, NC])
        xsum = sb("xsum", [P, NC])
        xrec = sb("xrec", [P, NC])
        xrv = sb("xrv", [P, NC])
        xp = [pr1[:, 0:2, :].rearrange("p a b -> p (a b)"), pr1[:, 2:4, :].rearrange("p a b -> p (a b)")]
        xpt = [pt1[:, 0], pt1[:, 1]]

        logits = sb("logits", [P, NC, E])
        top8 = sb("top8", [P, NC, 8])
        gt = sb("gt", [P, NC, E])
        eq = sb("eq", [P, NC, E])
        rank = sb("rank", [P, NC, E])
        need = sb("need", [P, NC])
        cnt = sb("cnt", [P, NC])
        within = sb("within", [P, NC, E])
        sel_eq = sb("sel_eq", [P, NC, E])
        sel = sb("sel", [P, NC, E])
        dlog = sb("dlog", [P, NC, E])
        elog = sb("elog", [P, NC, E])
        esel = sb("esel", [P, NC, E])
        etot = sb("etot", [P, NC])
        erec = sb("erec", [P, NC])
        score = sb("score", [P, NC, E])
        scoreT = sb("scoreT", [E, T])

        XH = sb("XH", [P, KD, T], F32R)
        XL = sb("XL", [P, KD, T], F32R)
        WHg = [sb(f"WHg{i}", [P, KD, 2, F], F32R) for i in range(2)]
        WLg = [sb(f"WLg{i}", [P, KD, 2, F], F32R) for i in range(2)]
        WHd = [sb(f"WHd{i}", [P, KD, D], F32R) for i in range(2)]
        WLd = [sb(f"WLd{i}", [P, KD, D], F32R) for i in range(2)]
        HH = [sb(f"HH{i}", [P, KD, T], F32R) for i in range(2)]
        HL = [sb(f"HL{i}", [P, KD, T], F32R) for i in range(2)]
        bup1 = sb("bup1", [P, E, 2])
        gcl, sig, glu, upc, hid = (kblk[:, i // 2, 4 * (i % 2):4 * (i % 2) + 4, :].rearrange("p (m h) s -> p m (h s)", m=2)
                                   for i in range(5))
        acc = x3

        x_in, qkv_in, param_in, row_in, ctx_in, ctxT_in, wo_in, mask_in, dbias_in = (
            sem(n) for n in ("x_in", "qkv_in", "param_in", "row_in", "ctx_in", "ctxT_in", "wo_in", "mask_in", "dbias_in"))
        raw_in = [sem(f"raw_in{i}") for i in range(2)]
        const_step, const_done = sem("const_step"), sem("const_done")
        dve_step = sem("dve_step")
        stat_done, lnv_done, rstd0_done, xn_done = sem("stat_done"), sem("lnv_done"), sem("rstd0_done"), sem("xn_done")
        lnT_done, xT0_done, xT1_done = sem("lnT_done"), sem("xT0_done"), sem("xT1_done")
        q_ps, k_ps, v_ps = sem("q_ps"), sem("k_ps"), sem("v_ps")
        q_done, k_done, v_done = sem("q_done"), sem("k_done"), sem("v_done")
        kblk_dve, kblk_pool = sem("kblk_dve"), sem("kblk_pool")
        sc_done, max_done, exp_done, pT_done = sem("sc_done"), sem("max_done"), sem("exp_done"), sem("pT_done")
        pt0_done, pt1_done, av_done, o_done = sem("pt0_done"), sem("pt1_done"), sem("av_done"), sem("o_done")
        ssum_done, att_done, proj_done = sem("ssum_done"), sem("att_done"), sem("proj_done")
        pen_done, valid_ps, valid_done = sem("pen_done"), sem("valid_ps"), sem("valid_done")
        xs_done, xbias_done, xexp_done, xpT_done = sem("xs_done"), sem("xbias_done"), sem("xexp_done"), sem("xpT_done")
        xpt_done, xav_done, x3_done = sem("xpt_done"), sem("xav_done"), sem("x3_done")
        xh_done, xl_done = sem("xh_done"), sem("xl_done")
        logit_ps, dlog_done, elog_done, score_done = sem("logit_ps"), sem("dlog_done"), sem("elog_done"), sem("score_done")
        scoreT_ps, scoreT_done, dbias_ps = sem("scoreT_ps"), sem("scoreT_done"), sem("dbias_ps")
        whg_done, wlg_done, whd_done, wld_done = sem("whg_done"), sem("wlg_done"), sem("whd_done"), sem("wld_done")
        gu_done, gcl_done, upc_done, sig_done, glu_done = (
            sem(n) for n in ("gu_done", "gcl_done", "upc_done", "sig_done", "glu_done"))
        hid_done, hh_done, hl_done, y_done, acc_done = (
            sem(n) for n in ("hid_done", "hh_done", "hl_done", "y_done", "acc_done"))
        out_done = sem("out_done")

        block = ctx.enter_context(nc.Block())

        def wait(eng, s, value):
            if not isinstance(value, int) or value > 0:
                eng.wait_ge(s, value)

        def all_experts(eng, body):
            for e in (0, 1):
                body(e, e, 0)
            with eng.Fori(1, E // 2 - 1) as pair:
                for slot in (0, 1):
                    body(pair * 2 + slot, slot, pair)
            for e in (E - 2, E - 1):
                body(e, e % 2, e // 2)

        xv = x_d.rearrange("b (c p) d -> p (b c) d", p=P)
        ov = out_d.rearrange("b (c p) d -> p (b c) d", p=P)

        @block.sync
        def _(sp):
            sp.dma_start(x[:, :, :], xv).then_inc(x_in, 16)
            sp.dma_start(wqkv[:, :, :, :], wqkv_d).then_inc(qkv_in, 16)
            for e in range(2):
                sp.dma_start(raw[e][:, :], we_d[e]).then_inc(raw_in[e], 16)
            sp.dma_start(wo[:, :, :], wo_d).then_inc(wo_in, 16)
            sp.dma_start(ctxT[:, :, :], ctxT_d).then_inc(ctxT_in, 16)
            sp.dma_start(ctx_sb[:, :, :], ctx_d.rearrange("b (c p) d -> p (b c) d", p=P)).then_inc(ctx_in, 16)
            with sp.Fori(1, E // 2) as pair:
                for slot in (0, 1):
                    sp.wait_ge(wlg_done, pair * 2 + slot - 1)
                    sp.wait_ge(wld_done, pair * 2 + slot - 1)
                    sp.dma_start(raw[slot][:, :], we_d[bass.ts(pair * 2 + slot, 1)].rearrange("e p n -> p (e n)")
                                 ).then_inc(raw_in[slot], 16)
            for c in range(NC):
                sp.wait_ge(acc_done, NC * (E + 1) - NC + c + 1)
                sp.dma_start(ov[:, c, :], acc[:, c, :]).then_inc(out_done, 16)
            sp.wait_ge(out_done, 16 * NC)

        @block.gpsimd
        def _(pool):
            step = [0]

            def link(ins):
                step[0] += 1
                ins.then_inc(const_step, 1)
                pool.wait_ge(const_step, step[0])

            g = nc.gpsimd
            g.memset(eps_t[:, :], EPS)
            link(g.memset(ident[:, :], 0.0))
            link(g.affine_select(out=ident[:, :], in_=ident[:, :], compare_op=ALU.not_equal, fill=1.0, base=0,
                                 pattern=[[-1, P]], channel_multiplier=1))
            link(g.memset(causal[:, :], 0.0))
            link(g.affine_select(out=causal[:, :], in_=causal[:, :], compare_op=ALU.is_ge, fill=NEG, base=0,
                                 pattern=[[-1, P]], channel_multiplier=1))
            g.tensor_copy(ident_bf[:, :], ident[:, :])
            link(g.memset(headmask[:, :], 1.0))
            link(g.affine_select(out=headmask[:, :], in_=headmask[:, :], compare_op=ALU.is_ge, fill=0.0, base=0,
                                 pattern=[[-DH, G8]], channel_multiplier=1))
            link(g.affine_select(out=headmask[:, :], in_=headmask[:, :], compare_op=ALU.is_ge, fill=0.0, base=DH - 1,
                                 pattern=[[DH, G8]], channel_multiplier=-1))
            link(g.memset(sumsel[:, :], 0.0))
            link(g.affine_select(out=sumsel[:, :].rearrange("p (j i) -> p j i", i=HP),
                                 in_=sumsel[:, :].rearrange("p (j i) -> p j i", i=HP), compare_op=ALU.not_equal,
                                 fill=1.0, base=-DH, pattern=[[-HP, P // HP], [0, HP]], channel_multiplier=1))
            g.memset(ones_bf[:, :], 1.0)
            g.memset(ones_f[:, :], 1.0)
            g.memset(one1[:, :], 1.0)
            g.memset(vp[:, :, :, DH:HP], 1.0)
            pool.wait_ge(row_in, 16)
            pool.wait_ge(x_in, 16)
            for c in range(NC):
                i = g.tensor_tensor(xb[:, c, :], x[:, c, :], bo_b, ALU.add)
            i.then_inc(const_done, 1)

            for k in range(KD):
                pool.wait_ge(k_done, k + 1)
                for h in range(G8):
                    i = g.tensor_scalar(kblk[:, KD + k, h, :], kT[:, k, S:T], headmask[:, h:h + 1], None, ALU.mult)
                i.then_inc(kblk_pool, 1)

            def low_gate_up(e, slot):
                wait(pool, whg_done, e + 1)
                wait(pool, gu_done, (e - 1) * 4)
                g.tensor_tensor(WLg[slot][:, :, :, :].rearrange("p k g f -> p (k g f)"), raw[slot][:, 0:GU],
                                WHg[slot][:, :, :, :].rearrange("p k g f -> p (k g f)").bitcast(F32), ALU.subtract
                                ).then_inc(wlg_done, 1)

            def low_down(e, slot):
                wait(pool, whd_done, e + 1)
                wait(pool, y_done, (e - 1) * 2)
                g.tensor_tensor(WLd[slot][:, :, :].rearrange("p k d -> p (k d)"), raw[slot][:, GU:GU + DW],
                                WHd[slot][:, :, :].rearrange("p k d -> p (k d)").bitcast(F32), ALU.subtract
                                ).then_inc(wld_done, 1)

            low_gate_up(0, 0)
            low_down(0, 0)
            low_gate_up(1, 1)

            def expert(e, slot, pair):
                for m in range(2):
                    pool.wait_ge(sig_done, e * 2 + (m + 1))
                    wait(pool, hid_done, e * 2 + (m - 1))
                    g.tensor_tensor(glu[:, m, :], gcl[:, m, :], sig[:, m, :], ALU.mult).then_inc(glu_done, 1)
                if not isinstance(e, int) or e + 2 < E:
                    low_gate_up(e + 2, slot)
                if not isinstance(e, int) or e + 1 < E:
                    low_down(e + 1, 1 - slot)

            all_experts(pool, expert)

        @block.scalar
        def _(act):
            a = nc.scalar
            act.dma_start(rows[:, :], rows_d.rearrange("(a n) -> a n", a=1).to_broadcast([P, 2 * D + E])).then_inc(row_in, 16)
            act.dma_start(params[:, :], params_d).then_inc(param_in, 16)
            act.dma_start(mask8[:, :], mask_d.rearrange("(a n) -> a n", a=1)).then_inc(mask_in, 16)
            act.dma_start(dbias[:, :], dbias_d).then_inc(dbias_in, 16)
            a.preload_act_table_set("natural_log_exp_and_others")

            def norm_seed(n):
                act.wait_ge(stat_done, n + 1)
                a.activation(lnv[:, :], ve[:, :], ACT.Ln).then_inc(lnv_done, 1)
                act.wait_ge(lnv_done, n + 1)
                a.activation(rstd0[:, :], lnv[:, :], ACT.Exp, scale=-0.5).then_inc(rstd0_done, 1)

            norm_seed(0)
            act.wait_ge(lnT_done, 2)
            a.activation(xT[:, 1, :], PS[:, 1, :], ACT.Copy).then_inc(xT1_done, 1)

            def exps(v):
                u, qc = divmod(v, 2)
                act.wait_ge(max_done, v + 1)
                if v >= 2:
                    act.wait_ge(pT_done, v - 1)
                for h in range(HG):
                    if qc == 0:
                        i = a.activation(pr0[:, h, :], PS[:, 0, h * P:(h + 1) * P], ACT.Exp, bias=nmax[:, 0, h:h + 1])
                    else:
                        i = a.activation(pr1[:, h, :], PS[:, 1 + h // 2, (h % 2) * S:(h % 2 + 1) * S], ACT.Exp,
                                         bias=nmax[:, 1, h:h + 1])
                i.then_inc(exp_done, 1)

            NV = 2 * B * NG
            for v in range(NV + 2):
                if v < NV:
                    exps(v)
                if 1 <= v <= NV and (v - 1) % 2 == 1:
                    w = v - 1
                    act.wait_ge(pT_done, w + 1)
                    if w >= 2:
                        act.wait_ge(av_done, w - 1)
                    a.activation(pt1[:, :, :, :].rearrange("p c h q -> p (c h q)"),
                                 PS[:, 4:6, :].rearrange("p b n -> p (b n)"), ACT.Copy).then_inc(pt1_done, 1)
                if v >= 2 and (v - 2) % 2 == 1:
                    u = (v - 2) // 2
                    b, hg = divmod(u, NG)
                    act.wait_ge(av_done, 2 * u + 2)
                    a.activation(osum[:, hg, b * S:(b + 1) * S], PS[:, 6 + u % 2, 0:S], ACT.Copy).then_inc(o_done, 1)

            def high_gate_up(e, slot, pair):
                act.wait_ge(raw_in[slot], pair * 16 + 16)
                wait(act, gu_done, (e - 1) * 4)
                a.activation(WHg[slot][:, :, :, :].rearrange("p k g f -> p (k g f)"), raw[slot][:, 0:GU], ACT.Copy
                             ).then_inc(whg_done, 1)

            def high_down(e, slot, pair):
                act.wait_ge(raw_in[slot], pair * 16 + 16)
                wait(act, y_done, (e - 1) * 2)
                a.activation(WHd[slot][:, :, :].rearrange("p k d -> p (k d)"), raw[slot][:, GU:GU + DW], ACT.Copy
                             ).then_inc(whd_done, 1)

            high_gate_up(0, 0, 0)
            high_down(0, 0, 0)
            high_gate_up(1, 1, 0)

            norm_seed(1)
            act.wait_ge(lnT_done, 4)
            a.activation(xT[:, 1, :], PS[:, 3, :], ACT.Copy).then_inc(xT1_done, 1)

            for c in range(NC + 1):
                if c < NC:
                    act.wait_ge(xbias_done, c + 1)
                    if c >= 2:
                        act.wait_ge(xpT_done, c - 1)
                    a.activation(xp[c % 2], PS[:, 4 + c % 2, :], ACT.Exp, bias=xbias[:, c:c + 1], scale=D ** -0.5,
                                 accum_out=xsum[:, c:c + 1]).then_inc(xexp_done, 1)
                if c >= 1:
                    w = c - 1
                    act.wait_ge(xpT_done, w + 1)
                    if w >= 2:
                        act.wait_ge(xav_done, w - 1)
                    a.activation(xpt[w % 2].rearrange("p h q -> p (h q)"), PS[:, 6 + w % 2, :], ACT.Copy
                                 ).then_inc(xpt_done, 1)

            norm_seed(2)
            act.wait_ge(lnT_done, 6)
            a.activation(xT[:, 1, :], PS[:, 3, :], ACT.Copy).then_inc(xT1_done, 1)
            for k in range(KD):
                act.wait_ge((xT0_done, xT1_done)[k], 3)
                a.activation(XH[:, k, :], xT[:, k, :], ACT.Copy).then_inc(xh_done, 1)
            act.wait_ge(dlog_done, 1)
            a.activation(elog[:, :, :], dlog[:, :, :], ACT.Exp).then_inc(elog_done, 1)

            def expert(e, slot, pair):
                for m in range(2):
                    act.wait_ge(gcl_done, e * 2 + (m + 1))
                    wait(act, glu_done, e * 2 + (m - 1))
                    a.activation(sig[:, m, :], gcl[:, m, :], ACT.Sigmoid, scale=ALPHA).then_inc(sig_done, 1)
                    act.wait_ge(hid_done, e * 2 + (m + 1))
                    wait(act, y_done, (e - 1) * 2)
                    a.activation(HH[slot][:, m, :], hid[:, m, :], ACT.Copy).then_inc(hh_done, 1)
                if not isinstance(e, int) or e + 2 < E:
                    high_gate_up(e + 2, slot, pair + 1)
                if not isinstance(e, int) or e + 1 < E:
                    high_down(e + 1, 1 - slot, pair + slot)

            all_experts(act, expert)

        @block.vector
        def _(dve):
            v_ = nc.vector
            step = [0]

            def link(ins):
                step[0] += 1
                ins.then_inc(dve_step, 1)
                dve.wait_ge(dve_step, step[0])

            def norm(src, n):
                for c in range(NC):
                    i = v_.bn_stats(stats[:, c, :], src[:, c, :])
                link(i)
                for c in range(NC):
                    i = v_.bn_aggr(mv[:, c, :], stats[:, c, :])
                link(i)
                v_.tensor_scalar(ve[:, :], mv[:, :, 1], EPS, None, ALU.add).then_inc(stat_done, 1)
                dve.wait_ge(rstd0_done, n + 1)
                link(v_.tensor_tensor(nw[:, 0, :], rstd0[:, :], rstd0[:, :], ALU.mult))
                link(v_.tensor_tensor(nw[:, 1, :], nw[:, 0, :], ve[:, :], ALU.mult))
                link(v_.tensor_scalar(nw[:, 2, :], nw[:, 1, :], -0.5, 1.5, ALU.mult, ALU.add))
                link(v_.tensor_tensor(rstd[:, :], nw[:, 2, :], rstd0[:, :], ALU.mult))
                for c in range(NC):
                    v_.tensor_scalar(xn[:, c, :], src[:, c, :], mv[:, c, 0:1], rstd[:, c:c + 1], ALU.subtract, ALU.mult
                                     ).then_inc(xn_done, 1)

            dve.wait_ge(x_in, 16)
            norm(x, 0)
            dve.wait_ge(lnT_done, 1)
            v_.tensor_copy(xT[:, 0, :], PS[:, 0, :]).then_inc(xT0_done, 1)
            dve.wait_ge(param_in, 16)
            v_.tensor_scalar(bup1[:, :, :], gub[:, :, 1, :], 1.0, None, ALU.add)
            for m in range(KD):
                dve.wait_ge(q_ps, m + 1)
                v_.tensor_scalar(qT[:, m, :], PS[:, 2 + m, :], bq[:, m:m + 1], DH ** -0.25, ALU.add, ALU.mult
                                 ).then_inc(q_done, 1)
            for m in range(KD):
                dve.wait_ge(k_ps, m + 1)
                v_.tensor_scalar(kT[:, m, :], PS[:, 4 + m, :], bk[:, m:m + 1], DH ** -0.25, ALU.add, ALU.mult
                                 ).then_inc(k_done, 1)
            for k in range(KD):
                dve.wait_ge(k_done, k + 1)
                dve.wait_ge(const_done, 1)
                for h in range(G8):
                    i = v_.tensor_scalar(kblk[:, k, h, :], kT[:, k, 0:S], headmask[:, h:h + 1], None, ALU.mult)
                i.then_inc(kblk_dve, 1)
            dve.wait_ge(row_in, 16)
            for c in range(NC):
                dve.wait_ge(v_ps, c // 2 * 2 + 2)
                v_.tensor_tensor(vp[:, c, :, 0:DH], PS[:, 6 + c // 2, (c % 2) * D:(c % 2 + 1) * D].rearrange("p (h d) -> p h d", d=DH),
                                 bv_b.rearrange("p (h d) -> p h d", d=DH), ALU.add).then_inc(v_done, 1)
            dve.wait_ge(mask_in, 16)
            link(v_.tensor_copy(maskf[:, :], mask8[:, :]))
            v_.tensor_scalar(pen[:, :], maskf[:, :], -1.0, -NEG, ALU.add, ALU.mult).then_inc(pen_done, 1)
            v_.tensor_reduce(valid1[:, :], maskf[:, :].rearrange("p (b m) -> p b m", b=B), AX.X, ALU.max).then_inc(pen_done, 1)

            NV = 2 * B * NG
            for v in range(NV + 3):
                if v < NV:
                    dve.wait_ge(sc_done, v + 1)
                    if v >= 2:
                        dve.wait_ge(exp_done, v - 1)
                    src = (PS[:, 0, :].rearrange("p (h k) -> p h k", h=HG) if v % 2 == 0 else
                           PS[:, 1:3, :].rearrange("p b (h k) -> p (b h) k", k=S))
                    v_.tensor_reduce(nmax[:, v % 2, :], src, AX.X, ALU.max, negate=True).then_inc(max_done, 1)
                if 1 <= v <= NV and (v - 1) % 2 == 0:
                    w = v - 1
                    dve.wait_ge(pT_done, w + 1)
                    if w >= 2:
                        dve.wait_ge(av_done, w - 1)
                    v_.tensor_copy(pt0[:, :, :].rearrange("p h q -> p (h q)"), PS[:, 3, :]).then_inc(pt0_done, 1)
                if v >= 3 and (v - 3) % 2 == 1:
                    u = (v - 3) // 2
                    b, hg = divmod(u, NG)
                    dve.wait_ge(ssum_done, u + 1)
                    link(v_.reciprocal(rsum[:, u % 2, :], PS[:, 6 + u % 2, S:2 * S]))
                    v_.tensor_tensor(attT[:, hg, b * S:(b + 1) * S], osum[:, hg, b * S:(b + 1) * S], rsum[:, u % 2, :],
                                     ALU.mult).then_inc(att_done, 1)
            dve.wait_ge(const_done, 1)
            for c in range(NC):
                dve.wait_ge(proj_done, c + 1)
                i = v_.tensor_tensor(x2[:, c, :], PS[:, c, 0:D], xb[:, c, :], ALU.add)
            link(i)
            norm(x2, 1)
            dve.wait_ge(lnT_done, 3)
            v_.tensor_copy(xT[:, 0, :], PS[:, 2, :]).then_inc(xT0_done, 1)
            dve.wait_ge(valid_ps, 1)
            v_.tensor_copy(valid[:, :], PS[:, 0, 0:B]).then_inc(valid_done, 1)
            dve.wait_ge(valid_done, 1)
            for c in range(NC + 2):
                if c < NC:
                    dve.wait_ge(xs_done, c + 1)
                    link(v_.tensor_reduce(xmax[:, c:c + 1], PS[:, 4 + c % 2, :], AX.X, ALU.max))
                    v_.tensor_scalar(xbias[:, c:c + 1], xmax[:, c:c + 1], -(D ** -0.5), None, ALU.mult
                                     ).then_inc(xbias_done, 1)
                if c >= 2:
                    w = c - 2
                    dve.wait_ge(xexp_done, w + 1)
                    link(v_.reciprocal(xrec[:, w:w + 1], xsum[:, w:w + 1]))
                    link(v_.tensor_tensor(xrv[:, w:w + 1], xrec[:, w:w + 1], valid[:, w // QC:w // QC + 1], ALU.mult))
                    dve.wait_ge(xav_done, w + 1)
                    v_.scalar_tensor_tensor(out=x3[:, w, :], in0=PS[:, w % 2, 0:D], scalar=xrv[:, w:w + 1],
                                            in1=x2[:, w, :], op0=ALU.mult, op1=ALU.add).then_inc(x3_done, 1)
            dve.wait_ge(x3_done, NC)
            norm(x3, 2)
            dve.wait_ge(lnT_done, 5)
            v_.tensor_copy(xT[:, 0, :], PS[:, 2, :]).then_inc(xT0_done, 1)
            for k in range(KD):
                dve.wait_ge(xh_done, k + 1)
                v_.tensor_tensor(XL[:, k, :], xT[:, k, :], XH[:, k, :].bitcast(F32), ALU.subtract).then_inc(xl_done, 1)

            dve.wait_ge(logit_ps, 1)
            link(v_.tensor_tensor(logits[:, :, :], PS[:, 4, 0:NC * E].rearrange("p (c e) -> p c e", e=E),
                                  rb_b.unsqueeze(1).to_broadcast([P, NC, E]), ALU.add))
            for c in range(NC):
                i = v_.max(top8[:, c, :], logits[:, c, :])
            link(i)
            kth = top8[:, :, TOP_K - 1:TOP_K].to_broadcast([P, NC, E])
            v_.tensor_tensor(dlog[:, :, :], logits[:, :, :], top8[:, :, 0:1].to_broadcast([P, NC, E]), ALU.subtract
                             ).then_inc(dlog_done, 1)
            v_.tensor_tensor(gt[:, :, :], logits[:, :, :], kth, ALU.is_gt)
            link(v_.tensor_tensor(eq[:, :, :], logits[:, :, :], kth, ALU.is_equal))
            link(v_.tensor_reduce(cnt[:, :], gt[:, :, :], AX.X, ALU.add))
            v_.tensor_scalar(need[:, :], cnt[:, :], -1.0, float(TOP_K), ALU.mult, ALU.add)
            for c in range(NC):
                i = v_.tensor_tensor_scan(rank[:, c, :], ones_f[:, :], eq[:, c, :], 0.0, ALU.mult, ALU.add)
            link(i)
            link(v_.tensor_tensor(within[:, :, :], rank[:, :, :], need[:, :].unsqueeze(2).to_broadcast([P, NC, E]), ALU.is_le))
            link(v_.tensor_tensor(sel_eq[:, :, :], eq[:, :, :], within[:, :, :], ALU.mult))
            link(v_.tensor_tensor(sel[:, :, :], sel_eq[:, :, :], gt[:, :, :], ALU.add))
            dve.wait_ge(elog_done, 1)
            link(v_.tensor_tensor(esel[:, :, :], elog[:, :, :], sel[:, :, :], ALU.mult))
            link(v_.tensor_reduce(etot[:, :], esel[:, :, :], AX.X, ALU.add))
            link(v_.reciprocal(erec[:, :], etot[:, :]))
            v_.tensor_tensor(score[:, :, :], esel[:, :, :], erec[:, :].unsqueeze(2).to_broadcast([P, NC, E]), ALU.mult
                             ).then_inc(score_done, 1)

            dve.wait_ge(scoreT_ps, 1)
            v_.tensor_copy(scoreT[:, :], PS[0:E, 5, :]).then_inc(scoreT_done, 1)

            def weighted_sum(e, slot):
                for c in range(NC):
                    if c % 2 == 0:
                        dve.wait_ge(y_done, e * 2 + (c // 2 + 1))
                    dve.wait_ge(acc_done, e * NC + (c + 1))
                    v_.scalar_tensor_tensor(out=acc[:, c, :], in0=PS[:, 4 + 2 * slot + c // 2, (c % 2) * D:(c % 2 + 1) * D],
                                            scalar=score[:, c, bass.ds(e, 1)], in1=acc[:, c, :], op0=ALU.mult, op1=ALU.add
                                            ).then_inc(acc_done, 1)

            def expert(e, slot, pair):
                def clamp_gate(m):
                    dve.wait_ge(gu_done, e * 4 + (2 * m + 1))
                    wait(dve, glu_done, e * 2 + (m - 1))
                    v_.tensor_scalar(gcl[:, m, :], PS[:, 2 * m, :], gub[:, bass.ds(e, 1), 0, m], LIMIT, ALU.add, ALU.min
                                     ).then_inc(gcl_done, 1)

                def clamp_up(m):
                    dve.wait_ge(gu_done, e * 4 + (2 * m + 2))
                    wait(dve, hid_done, e * 2 + (m - 1))
                    v_.tensor_scalar(upc[:, m, :], PS[:, 2 * m + 1, :], bup1[:, bass.ds(e, 1), m], 1.0 - LIMIT, ALU.add, ALU.max
                                     ).then_inc(upc_done, 1)

                def product(m):
                    dve.wait_ge(glu_done, e * 2 + (m + 1))
                    dve.wait_ge(upc_done, e * 2 + (m + 1))
                    wait(dve, hl_done, e * 2 + (m - 1))
                    v_.scalar_tensor_tensor(out=hid[:, m, :], in0=upc[:, m, :], scalar=1.0 + LIMIT, in1=glu[:, m, :],
                                            op0=ALU.min, op1=ALU.mult).then_inc(hid_done, 1)

                def low(m):
                    dve.wait_ge(hh_done, e * 2 + (m + 1))
                    v_.tensor_tensor(HL[slot][:, m, :], hid[:, m, :], HH[slot][:, m, :].bitcast(F32), ALU.subtract
                                     ).then_inc(hl_done, 1)

                clamp_gate(0)
                clamp_up(0)
                product(0)
                clamp_gate(1)
                low(0)
                clamp_up(1)
                product(1)
                low(1)
                if isinstance(e, int) and e == 0:
                    for c in range(NC):
                        dve.wait_ge(dbias_ps, c // 2 * 2 + 2)
                        v_.tensor_tensor(acc[:, c, :], PS[:, 6 + c // 2, (c % 2) * D:(c % 2 + 1) * D], x3[:, c, :], ALU.add
                                         ).then_inc(acc_done, 1)
                else:
                    weighted_sum(e - 1, 1 - slot)

            all_experts(dve, expert)
            weighted_sum(E - 1, (E - 1) % 2)

        @block.tensor
        def _(pe):
            t = nc.tensor

            def transposes(n, bank):
                for k in range(KD):
                    for c in range(NC):
                        if k == 0:
                            pe.wait_ge(xn_done, n * NC + c + 1)
                        i = t.transpose(PS[:, bank + k, c * P:(c + 1) * P], xn[:, c, k * P:(k + 1) * P], ident[:, :])
                    i.then_inc(lnT_done, 1)

            pe.wait_ge(const_done, 1)
            transposes(0, 0)
            pe.wait_ge(qkv_in, 16)
            pe.wait_ge(xT0_done, 1)
            pe.wait_ge(xT1_done, 1)
            for j, (bank, done) in enumerate(((2, q_ps), (4, k_ps))):
                for m in range(KD):
                    for k in range(KD):
                        i = t.matmul(PS[:, bank + m, :], wqkv[:, j, k, m * P:(m + 1) * P], xT[:, k, :], start=(k == 0), stop=(k == KD - 1))
                    i.then_inc(done, 1)
            for c in range(NC):
                for k in range(KD):
                    i = t.matmul(PS[:, 6 + c // 2, (c % 2) * D:(c % 2 + 1) * D], xT[:, k, c * P:(c + 1) * P], wqkv[:, 2, k, :],
                                 start=(k == 0), stop=(k == KD - 1))
                i.then_inc(v_ps, 1)

            NV = 2 * B * NG
            pe.wait_ge(q_done, KD)

            def scores(v):
                u, qc = divmod(v, 2)
                b, hg = divmod(u, NG)
                g, h0 = hg // 2, (hg % 2) * HG
                if b == 0:
                    pe.wait_ge(kblk_dve, g + 1)
                else:
                    pe.wait_ge(kblk_pool, g + 1)
                if v >= 2:
                    pe.wait_ge(exp_done, v - 1)
                q = qT[:, g, b * S + qc * P:b * S + (qc + 1) * P]
                keys = kblk[:, b * KD + g]
                if qc == 0:
                    out = PS[:, 0, :].rearrange("p (h k) -> p h k", h=HG)
                    t.matmul(out, q, keys[:, h0:h0 + HG, 0:P], start=True, stop=False)
                    i = t.matmul(out, ident_bf[:, :], causal[:, :].unsqueeze(1).to_broadcast([P, HG, P]), start=False, stop=True)
                else:
                    for j in range(2):
                        out = PS[:, 1 + j, :].rearrange("p (h k) -> p h k", h=2)
                        t.matmul(out, q, keys[:, h0 + 2 * j:h0 + 2 * j + 2, :], start=True, stop=False)
                        i = t.matmul(out[:, :, P:S], ident_bf[:, :], causal[:, :].unsqueeze(1).to_broadcast([P, 2, P]),
                                     start=False, stop=True)
                i.then_inc(sc_done, 1)

            def turn(v):
                pe.wait_ge(exp_done, v + 1)
                if v % 2 == 0:
                    if v >= 2:
                        pe.wait_ge(pt0_done, v // 2)
                    for h in range(HG):
                        i = t.transpose(PS[:, 3, h * P:(h + 1) * P], pr0[:, h, :], ident[:, :])
                else:
                    if v >= 2:
                        pe.wait_ge(pt1_done, v // 2)
                    for kc in range(QC):
                        for h in range(HG):
                            i = t.transpose(PS[:, 4 + kc, h * P:(h + 1) * P], pr1[:, h, kc * P:(kc + 1) * P], ident[:, :])
                i.then_inc(pT_done, 1)

            def values(v):
                u, qc = divmod(v, 2)
                b, hg = divmod(u, NG)
                if v == 0:
                    pe.wait_ge(v_done, NC)
                if qc == 0:
                    pe.wait_ge(pt0_done, u + 1)
                    if u >= 2:
                        pe.wait_ge(att_done, u - 1)
                else:
                    pe.wait_ge(pt1_done, u + 1)
                for kc in range(qc + 1):
                    for h in range(HG):
                        p = pt0[:, h, :] if qc == 0 else pt1[:, kc, h, :]
                        i = t.matmul(PS[HP * h:HP * (h + 1), 6 + u % 2, qc * P:(qc + 1) * P], vp[:, b * QC + kc, hg * HG + h, :], p,
                                     start=(kc == 0), stop=(kc == qc))
                i.then_inc(av_done, 1)

            def spread_sums(u):
                b, hg = divmod(u, NG)
                pe.wait_ge(o_done, u + 1)
                t.matmul(PS[:, 6 + u % 2, S:2 * S], sumsel[:, :], osum[:, hg, b * S:(b + 1) * S], start=True, stop=True
                         ).then_inc(ssum_done, 1)

            for v in range(NV + 3):
                if v < NV:
                    scores(v)
                if 1 <= v <= NV:
                    turn(v - 1)
                if 2 <= v <= NV + 1:
                    values(v - 2)
                if v >= 3 and (v - 3) % 2 == 1:
                    spread_sums((v - 3) // 2)

            pe.wait_ge(wo_in, 16)
            for c in range(NC):
                pe.wait_ge(att_done, NG * (c // QC + 1))
                for hg in range(NG):
                    i = t.matmul(PS[:, c, 0:D], attT[:, hg, c * P:(c + 1) * P], wo[:, hg, :], start=(hg == 0), stop=(hg == NG - 1))
                i.then_inc(proj_done, 1)

            transposes(1, 2)
            pe.wait_ge(pen_done, 2)
            pe.wait_ge(ctxT_in, 16)
            t.matmul(PS[:, 0, 0:B], one1[:, :], valid1[:, :], start=True, stop=True).then_inc(valid_ps, 1)
            for c in range(NC + 2):
                if c < NC:
                    if c == 0:
                        pe.wait_ge(xT0_done, 2)
                        pe.wait_ge(xT1_done, 2)
                    if c >= 2:
                        pe.wait_ge(xexp_done, c - 1)
                    b = c // QC
                    for k in range(KD):
                        t.matmul(PS[:, 4 + c % 2, :], xT[:, k, c * P:(c + 1) * P], ctxT[:, b * KD + k, :], start=(k == 0), stop=False)
                    t.matmul(PS[:, 4 + c % 2, :], ones_bf[:, :], pen[:, b * M:(b + 1) * M], start=False, stop=True
                             ).then_inc(xs_done, 1)
                if 1 <= c <= NC:
                    w = c - 1
                    pe.wait_ge(xexp_done, w + 1)
                    if w >= 2:
                        pe.wait_ge(xpt_done, w - 1)
                    for j in range(KM):
                        i = t.transpose(PS[:, 6 + w % 2, j * P:(j + 1) * P], xp[w % 2][:, j * P:(j + 1) * P], ident[:, :])
                    i.then_inc(xpT_done, 1)
                if c >= 2:
                    w = c - 2
                    pe.wait_ge(xpt_done, w + 1)
                    if w == 0:
                        pe.wait_ge(ctx_in, 16)
                        pe.wait_ge(valid_done, 1)
                    if w >= 2:
                        pe.wait_ge(x3_done, w - 1)
                    for j in range(KM):
                        i = t.matmul(PS[:, w % 2, 0:D], xpt[w % 2][:, j, :], ctx_sb[:, (w // QC) * KM + j, :], start=(j == 0), stop=(j == KM - 1))
                    i.then_inc(xav_done, 1)

            transposes(2, 2)
            pe.wait_ge(xT0_done, 3)
            pe.wait_ge(xT1_done, 3)
            for c in range(NC):
                for k in range(KD):
                    i = t.matmul(PS[:, 4, c * E:(c + 1) * E], xT[:, k, c * P:(c + 1) * P], routerT[:, k, :], start=(k == 0), stop=(k == KD - 1))
            i.then_inc(logit_ps, 1)

            def gate_up(e, slot):
                pe.wait_ge(wlg_done, e + 1)
                for m in range(2):
                    for part in range(2):
                        wait(pe, gcl_done if part == 0 else upc_done, e * 2 + (m - 1))
                        n = 0
                        for k in range(KD):
                            for w, xx in ((WHg, XH), (WHg, XL), (WLg, XH)):
                                i = t.matmul(PS[:, 2 * m + part, :], w[slot][:, k, part, m * P:(m + 1) * P], xx[:, k, :],
                                             start=(n == 0), stop=(n == 3 * KD - 1))
                                n += 1
                        i.then_inc(gu_done, 1)

            def down(e, slot):
                pe.wait_ge(hl_done, e * 2 + 2)
                pe.wait_ge(wld_done, e + 1)
                wait(pe, acc_done, (e - 1) * NC)
                for c in range(NC):
                    n = 0
                    for k in range(KD):
                        for hh, w in ((HH, WHd), (HL, WHd), (HH, WLd)):
                            i = t.matmul(PS[:, 4 + 2 * slot + c // 2, (c % 2) * D:(c % 2 + 1) * D], hh[slot][:, k, c * P:(c + 1) * P],
                                         w[slot][:, k, :], start=(n == 0), stop=(n == 3 * KD - 1))
                            n += 1
                    if c % 2 == 1:
                        i.then_inc(y_done, 1)

            pe.wait_ge(xl_done, KD)
            gate_up(0, 0)
            pe.wait_ge(score_done, 1)
            for c in range(NC):
                i = t.transpose(PS[0:E, 5, c * P:(c + 1) * P], score[:, c, :], ident[:, :])
            i.then_inc(scoreT_ps, 1)
            pe.wait_ge(scoreT_done, 1)
            pe.wait_ge(dbias_in, 16)
            for c in range(NC):
                t.matmul(PS[:, 6 + c // 2, (c % 2) * D:(c % 2 + 1) * D], scoreT[:, c * P:(c + 1) * P], dbias[:, :], start=True, stop=True
                         ).then_inc(dbias_ps, 1)

            def both(e, slot, pair):
                if not isinstance(e, int) or e + 1 < E:
                    gate_up(e + 1, 1 - slot)
                down(e, slot)

            all_experts(pe, both)


def kernel(**inputs):
    import numpy as np
    import concourse.bacc as bacc
    from concourse.bass_utils import run_bass_kernel_spmd

    a = {n: np.ascontiguousarray(v) for n, v in inputs.items()}

    def rows_in(w):
        return w.reshape(-1, P, w.shape[-1]).transpose(1, 0, 2)

    wqkv = np.stack([rows_in(a[f"L0_attn_W{n}"].T) for n in "qkv"], axis=1)
    wo = np.zeros((NG, HG, HP, D), np.float32)
    wo[:, :, :DH, :] = a["L0_attn_Wo"].T.reshape(NG, HG, DH, D)
    wo = wo.reshape(NG, P, D).transpose(1, 0, 2)
    gub = a["L0_ffn_gate_up_proj_bias"].reshape(E, KD, P, 2).transpose(2, 0, 3, 1)
    params = np.concatenate([a["L0_attn_bq"].reshape(KD, P).T, a["L0_attn_bk"].reshape(KD, P).T, gub.reshape(P, -1),
                             rows_in(a["L0_ffn_router_weight"].T).reshape(P, -1)], axis=1)
    rows = np.concatenate([a["L0_attn_bv"], a["L0_attn_bo"], a["L0_ffn_router_bias"]])
    gup = a["L0_ffn_gate_up_proj"].reshape(E, KD, P, F, 2).transpose(0, 2, 1, 4, 3).reshape(E, P, GU)
    down = a["L0_ffn_down_proj"].reshape(E, KD, P, D).transpose(0, 2, 1, 3).reshape(E, P, DW)
    ctxT = a["ctx_2048"].transpose(2, 0, 1).reshape(KD, P, B, M).transpose(1, 2, 0, 3).reshape(P, B * KD, M)
    arrays = {
        "x_d": a["x"], "ctx_d": a["ctx_2048"], "ctxT_d": ctxT, "wqkv_d": wqkv, "wo_d": wo, "params_d": params,
        "rows_d": rows, "mask_d": a["mask_BxS2_bk0"].reshape(-1), "dbias_d": a["L0_ffn_down_proj_bias"],
        "we_d": np.concatenate([gup, down], axis=2),
    }
    arrays = {n: np.ascontiguousarray(v) for n, v in arrays.items()}
    nc = bacc.Bacc("TRN2", target_bir_lowering=False, num_devices=1)
    args = [nc.dram_tensor(n, v.shape, mybir.dt.from_np(v.dtype), kind="ExternalInput").ap() for n, v in arrays.items()]
    out = nc.dram_tensor("out_d", (B, S, D), F32, kind="ExternalOutput").ap()
    decoder_layer(nc, *args, out)
    got = run_bass_kernel_spmd(nc, [arrays], core_ids=[0])
    return got.results[0]["out_d"]
```

```python
from contextlib import ExitStack

import concourse.bass as bass
from concourse import mybir

F32 = mybir.dt.float32
F32R = mybir.dt.float32r
BF16 = mybir.dt.bfloat16
U8 = mybir.dt.uint8
ALU = mybir.AluOpType
ACT = mybir.ActivationFunctionType
AX = mybir.AxisListType

P = 128
B, S, D = 2, 256, 256
M = 512
H, DH = 16, 16
E, F = 16, 256
TOP_K = 4
T = B * S
NC = T // P
QC = S // P
KD = D // P
KM = M // P
HG = 4
NG = H // HG
G8 = P // DH
HP = 32
EPS = 1e-5
ALPHA, LIMIT = 1.702, 7.0
NEG = -1e30
GU = 2 * F * KD
DW = D * KD


def decoder_layer(nc, x_d, ctx_d, ctxT_d, wqkv_d, wo_d, params_d, rows_d, mask_d, dbias_d, we_d, out_d):
    ctx = ExitStack()
    with ctx:
        def sb(name, shape, dt=F32):
            return ctx.enter_context(nc.sbuf_tensor(name, shape, dt))

        def sem(name):
            return ctx.enter_context(nc.semaphore(name))

        PS = ctx.enter_context(nc.psum_tensor("PS", [P, 8, 512], F32))

        x = sb("x", [P, NC, D])
        ctx_sb = sb("ctx_sb", [P, B * KM, D])
        ctxT = sb("ctxT", [P, B * KD, M])
        wqkv = sb("wqkv", [P, 3, KD, D])
        wo = sb("wo", [P, KD, D])
        params = sb("params", [P, 4 + 4 * E + KD * E])
        rows = sb("rows", [P, 2 * D + E])
        mask8 = sb("mask8", [1, B * M], U8)
        dbias = sb("dbias", [E, D])
        raw_g = [sb(f"raw_g{i}", [P, GU]) for i in range(2)]
        raw_w = [sb(f"raw_w{i}", [P, DW]) for i in range(2)]
        bq, bk = params[:, 0:2], params[:, 2:4]
        gub = params[:, 4:4 + 4 * E].rearrange("p (e g m) -> p e g m", e=E, g=2)
        routerT = params[:, 4 + 4 * E:].rearrange("p (k e) -> p k e", k=KD)
        bv_b, bo_b, rb_b = rows[:, 0:D], rows[:, D:2 * D], rows[:, 2 * D:]

        ident = sb("ident", [P, P])
        ident_bf = sb("ident_bf", [P, P], BF16)
        causal = sb("causal", [P, P], BF16)
        headmask = sb("headmask", [P, G8])
        ones_bf = sb("ones_bf", [1, P], BF16)
        warm = sb("warm", [P, 512], BF16)
        half = sb("half", [P, NC])
        ones_f = sb("ones_f", [P, E])
        one1 = sb("one1", [1, P])

        xb = sb("xb", [P, NC, D])
        xn = sb("xn", [P, NC, D])
        xT = sb("xT", [P, KD, T])
        qT = sb("qT", [P, KD, T])
        kT = sb("kT", [P, KD, T])
        kblk = sb("kblk", [P, B * KD, G8, S])
        vp = sb("vp", [P, NC, H, HP])
        pr0 = sb("pr0", [P, HG, P])
        pr1 = sb("pr1", [P, HG, S])
        pt0 = sb("pt0", [P, HG, P])
        pt1 = sb("pt1", [P, QC, HG, P])
        nmax = sb("nmax", [P, 2, HG])
        osum = sb("osum", [P, NG, T])
        rsum = sb("rsum", [P, QC, H])
        att = sb("att", [P, NC, D])
        attT = sb("attT", [P, KD, T])
        x2 = sb("x2", [P, NC, D])
        x3 = sb("x3", [P, NC, D])
        stats = sb("stats", [P, NC, 6])
        mv = sb("mv", [P, NC, 2])
        ve = sb("ve", [P, NC])
        rstd = sb("rstd", [P, NC])
        maskf = sb("maskf", [1, B * M])
        pen = sb("pen", [1, B * M], BF16)
        valid1 = sb("valid1", [1, B])
        valid = sb("valid", [P, B])
        xmax = sb("xmax", [P, NC])
        xbias = sb("xbias", [P, NC])
        xsum = sb("xsum", [P, NC])
        xrec = sb("xrec", [P, NC])
        xrv = sb("xrv", [P, NC])
        xp = [pr1[:, 0:2, :].rearrange("p a b -> p (a b)"), pr1[:, 2:4, :].rearrange("p a b -> p (a b)")]
        xpt = [pt1[:, 0], pt1[:, 1]]

        logits = sb("logits", [P, NC, E])
        top8 = sb("top8", [P, NC, 8])
        gt = sb("gt", [P, NC, E])
        eq = sb("eq", [P, NC, E])
        rank = sb("rank", [P, NC, E])
        need = sb("need", [P, NC])
        cnt = sb("cnt", [P, NC])
        within = sb("within", [P, NC, E])
        sel_eq = sb("sel_eq", [P, NC, E])
        sel = sb("sel", [P, NC, E])
        dlog = sb("dlog", [P, NC, E])
        elog = sb("elog", [P, NC, E])
        esel = sb("esel", [P, NC, E])
        etot = sb("etot", [P, NC])
        erec = sb("erec", [P, NC])
        score = sb("score", [P, NC, E])
        scoreT = sb("scoreT", [E, T])

        XH = sb("XH", [P, KD, T], F32R)
        XL = sb("XL", [P, KD, T], F32R)
        WHg = [sb(f"WHg{i}", [P, KD, 2, F], F32R) for i in range(2)]
        WLg = [sb(f"WLg{i}", [P, KD, 2, F], F32R) for i in range(2)]
        WHd = [sb(f"WHd{i}", [P, KD, D], F32R) for i in range(2)]
        WLd = [sb(f"WLd{i}", [P, KD, D], F32R) for i in range(2)]
        HH = [sb(f"HH{i}", [P, KD, T], F32R) for i in range(2)]
        HL = [sb(f"HL{i}", [P, KD, T], F32R) for i in range(2)]
        bup1 = sb("bup1", [P, E, 2])
        gcl, sig, glu, upc, hid = (kblk[:, i // 2, 4 * (i % 2):4 * (i % 2) + 4, :].rearrange("p (m h) s -> p m (h s)", m=2)
                                   for i in range(5))
        acc = x3

        x_in, qkv_in, param_in, row_in, ctx_in, ctxT_in, wo_in, mask_in, dbias_in = (
            sem(n) for n in ("x_in", "qkv_in", "param_in", "row_in", "ctx_in", "ctxT_in", "wo_in", "mask_in", "dbias_in"))
        raw_g_in = [sem(f"raw_g_in{i}") for i in range(2)]
        raw_w_in = [sem(f"raw_w_in{i}") for i in range(2)]
        const_step, const_done, ident_done, warm_done = (sem(n) for n in ("const_step", "const_done", "ident_done", "warm_done"))
        dve_step = sem("dve_step")
        bn_done, stat_done, rstd_done, xn_done = sem("bn_done"), sem("stat_done"), sem("rstd_done"), sem("xn_done")
        lnT_done, xT0_done, xT1_done = sem("lnT_done"), sem("xT0_done"), sem("xT1_done")
        q_ps, k_ps, v_ps = sem("q_ps"), sem("k_ps"), sem("v_ps")
        q_done, k_done, v_done = sem("q_done"), sem("k_done"), sem("v_done")
        kblk_dve, kblk_pool = sem("kblk_dve"), sem("kblk_pool")
        sc_done, max_done, exp_done, pT_done = sem("sc_done"), sem("max_done"), sem("exp_done"), sem("pT_done")
        pt0_done, pt1_done, av_done, o_done = sem("pt0_done"), sem("pt1_done"), sem("av_done"), sem("o_done")
        back_done, att_done, attT0_done, attT1_done, proj_done = (
            sem(n) for n in ("back_done", "att_done", "attT0_done", "attT1_done", "proj_done"))
        pen_done, valid_ps, valid_done = sem("pen_done"), sem("valid_ps"), sem("valid_done")
        xs_done, xbias_done, xexp_done, xpT_done = sem("xs_done"), sem("xbias_done"), sem("xexp_done"), sem("xpT_done")
        xpt_done, xav_done, x3_done = sem("xpt_done"), sem("xav_done"), sem("x3_done")
        xh_done, xl_done = sem("xh_done"), sem("xl_done")
        logit_ps, dlog_done, elog_done, score_done = sem("logit_ps"), sem("dlog_done"), sem("elog_done"), sem("score_done")
        scoreT_ps, scoreT_done, dbias_ps = sem("scoreT_ps"), sem("scoreT_done"), sem("dbias_ps")
        whg_done, wlg_done, whd_done, wld_done = sem("whg_done"), sem("wlg_done"), sem("whd_done"), sem("wld_done")
        gu_done, gcl_done, upc_done, sig_done, glu_done = (
            sem(n) for n in ("gu_done", "gcl_done", "upc_done", "sig_done", "glu_done"))
        hid_done, hh_done, hl_done, y_done, acc_done = (
            sem(n) for n in ("hid_done", "hh_done", "hl_done", "y_done", "acc_done"))
        out_done = sem("out_done")

        block = ctx.enter_context(nc.Block())

        def wait(eng, s, value):
            if not isinstance(value, int) or value > 0:
                eng.wait_ge(s, value)

        def all_experts(eng, body):
            for e in (0, 1):
                body(e, e, 0)
            with eng.Fori(1, E // 2 - 1) as pair:
                for slot in (0, 1):
                    body(pair * 2 + slot, slot, pair)
            for e in (E - 2, E - 1):
                body(e, e % 2, e // 2)

        xv = x_d.rearrange("b (c p) d -> p (b c) d", p=P)
        ov = out_d.rearrange("b (c p) d -> p (b c) d", p=P)

        @block.sync
        def _(sp):
            sp.dma_start(x[:, :, :], xv).then_inc(x_in, 16)
            sp.dma_start(wqkv[:, :, :, :], wqkv_d).then_inc(qkv_in, 16)
            for e in range(2):
                sp.dma_start(raw_g[e][:, :], we_d[e, :, 0:GU]).then_inc(raw_g_in[e], 16)
                sp.dma_start(raw_w[e][:, :], we_d[e, :, GU:]).then_inc(raw_w_in[e], 16)
            sp.dma_start(wo[:, :, :], wo_d).then_inc(wo_in, 16)
            sp.dma_start(ctxT[:, :, :], ctxT_d).then_inc(ctxT_in, 16)
            sp.dma_start(ctx_sb[:, :, :], ctx_d.rearrange("b (c p) d -> p (b c) d", p=P)).then_inc(ctx_in, 16)
            with sp.Fori(1, E // 2) as pair:
                for slot in (0, 1):
                    sp.wait_ge(wlg_done, pair * 2 + slot - 1)
                    expert = we_d[bass.ts(pair * 2 + slot, 1)].rearrange("e p n -> p (e n)")
                    sp.dma_start(raw_g[slot][:, :], expert[:, 0:GU]).then_inc(raw_g_in[slot], 16)
                    sp.wait_ge(wld_done, pair * 2 + slot - 1)
                    sp.dma_start(raw_w[slot][:, :], expert[:, GU:]).then_inc(raw_w_in[slot], 16)
            for c in range(NC):
                sp.wait_ge(acc_done, NC * (E + 1) - NC + c + 1)
                sp.dma_start(ov[:, c, :], acc[:, c, :]).then_inc(out_done, 16)
            sp.wait_ge(out_done, 16 * NC)

        @block.gpsimd
        def _(pool):
            step = [0]

            def link(ins):
                step[0] += 1
                ins.then_inc(const_step, 1)
                pool.wait_ge(const_step, step[0])

            g = nc.gpsimd
            g.memset(warm[:, :], 0.0).then_inc(warm_done, 1)
            g.memset(half[:, :], -0.5)
            link(g.memset(ident[:, :], 0.0))
            g.affine_select(out=ident[:, :], in_=ident[:, :], compare_op=ALU.not_equal, fill=1.0, base=0,
                            pattern=[[-1, P]], channel_multiplier=1).then_inc(ident_done, 1)
            link(g.memset(causal[:, :], 0.0))
            link(g.affine_select(out=causal[:, :], in_=causal[:, :], compare_op=ALU.is_ge, fill=NEG, base=0,
                                 pattern=[[-1, P]], channel_multiplier=1))
            pool.wait_ge(ident_done, 1)
            g.tensor_copy(ident_bf[:, :], ident[:, :])
            link(g.memset(headmask[:, :], 1.0))
            link(g.affine_select(out=headmask[:, :], in_=headmask[:, :], compare_op=ALU.is_ge, fill=0.0, base=0,
                                 pattern=[[-DH, G8]], channel_multiplier=1))
            link(g.affine_select(out=headmask[:, :], in_=headmask[:, :], compare_op=ALU.is_ge, fill=0.0, base=DH - 1,
                                 pattern=[[DH, G8]], channel_multiplier=-1))
            g.memset(ones_bf[:, :], 1.0)
            g.memset(ones_f[:, :], 1.0)
            g.memset(one1[:, :], 1.0)
            g.memset(vp[:, :, :, DH:HP], 1.0)
            def rstds(n):
                pool.wait_ge(stat_done, n + 1)
                g.tensor_tensor(rstd[:, :], ve[:, :], half[:, :], ALU.pow).then_inc(rstd_done, 1)

            rstds(0)
            pool.wait_ge(row_in, 16)
            pool.wait_ge(x_in, 16)
            for c in range(NC):
                i = g.tensor_tensor(xb[:, c, :], x[:, c, :], bo_b, ALU.add)
            i.then_inc(const_done, 1)

            for k in range(KD):
                pool.wait_ge(k_done, k + 1)
                for h in range(G8):
                    i = g.tensor_scalar(kblk[:, KD + k, h, :], kT[:, k, S:T], headmask[:, h:h + 1], None, ALU.mult)
                i.then_inc(kblk_pool, 1)

            def low_gate_up(e, slot):
                wait(pool, whg_done, e + 1)
                wait(pool, gu_done, (e - 1) * 4)
                g.tensor_tensor(WLg[slot][:, :, :, :].rearrange("p k g f -> p (k g f)"), raw_g[slot][:, :],
                                WHg[slot][:, :, :, :].rearrange("p k g f -> p (k g f)").bitcast(F32), ALU.subtract
                                ).then_inc(wlg_done, 1)

            def low_down(e, slot):
                wait(pool, whd_done, e + 1)
                wait(pool, y_done, (e - 1) * 2)
                g.tensor_tensor(WLd[slot][:, :, :].rearrange("p k d -> p (k d)"), raw_w[slot][:, :],
                                WHd[slot][:, :, :].rearrange("p k d -> p (k d)").bitcast(F32), ALU.subtract
                                ).then_inc(wld_done, 1)

            low_gate_up(0, 0)
            low_down(0, 0)
            low_gate_up(1, 1)
            rstds(1)
            rstds(2)

            def expert(e, slot, pair):
                for m in range(2):
                    pool.wait_ge(sig_done, e * 2 + (m + 1))
                    wait(pool, hid_done, e * 2 + (m - 1))
                    g.tensor_tensor(glu[:, m, :], gcl[:, m, :], sig[:, m, :], ALU.mult).then_inc(glu_done, 1)
                if not isinstance(e, int) or e + 2 < E:
                    low_gate_up(e + 2, slot)
                if not isinstance(e, int) or e + 1 < E:
                    low_down(e + 1, 1 - slot)

            all_experts(pool, expert)

        @block.scalar
        def _(act):
            a = nc.scalar
            act.dma_start(rows[:, :], rows_d.rearrange("(a n) -> a n", a=1).to_broadcast([P, 2 * D + E])).then_inc(row_in, 16)
            act.dma_start(params[:, :], params_d).then_inc(param_in, 16)
            act.dma_start(mask8[:, :], mask_d.rearrange("(a n) -> a n", a=1)).then_inc(mask_in, 16)
            act.dma_start(dbias[:, :], dbias_d).then_inc(dbias_in, 16)
            a.preload_act_table_set("natural_log_exp_and_others")

            act.wait_ge(lnT_done, 2)
            a.activation(xT[:, :, S:T], PS[:, 1, :].rearrange("p (k n) -> p k n", k=KD), ACT.Copy).then_inc(xT1_done, 1)

            def high_gate_up(e, slot, pair):
                act.wait_ge(raw_g_in[slot], pair * 16 + 16)
                wait(act, gu_done, (e - 1) * 4)
                a.activation(WHg[slot][:, :, :, :].rearrange("p k g f -> p (k g f)"), raw_g[slot][:, :], ACT.Copy
                             ).then_inc(whg_done, 1)

            def high_down(e, slot, pair):
                act.wait_ge(raw_w_in[slot], pair * 16 + 16)
                wait(act, y_done, (e - 1) * 2)
                a.activation(WHd[slot][:, :, :].rearrange("p k d -> p (k d)"), raw_w[slot][:, :], ACT.Copy
                             ).then_inc(whd_done, 1)

            high_gate_up(0, 0, 0)
            high_down(0, 0, 0)
            high_gate_up(1, 1, 0)

            def exps(v):
                u, qc = divmod(v, 2)
                if v >= 2:
                    act.wait_ge(pT_done, v - 1)
                for h in range(HG):
                    if h % 2 == 0:
                        act.wait_ge(max_done, 3 * u + 1 + qc * (1 + h // 2))
                    if qc == 0:
                        i = a.activation(pr0[:, h, :], PS[:, 0, h * P:(h + 1) * P], ACT.Exp, bias=nmax[:, 0, h:h + 1])
                    else:
                        i = a.activation(pr1[:, h, :], PS[:, 1 + h // 2, (h % 2) * S:(h % 2 + 1) * S], ACT.Exp,
                                         bias=nmax[:, 1, h:h + 1])
                i.then_inc(exp_done, 1)

            NV = 2 * B * NG
            for v in range(NV + 2):
                if v < NV:
                    exps(v)
                if 1 <= v <= NV and (v - 1) % 2 == 1:
                    w = v - 1
                    act.wait_ge(pT_done, w + 1)
                    if w >= 2:
                        act.wait_ge(av_done, w - 1)
                    a.activation(pt1[:, :, :, :].rearrange("p c h q -> p (c h q)"),
                                 PS[:, 4:6, :].rearrange("p b n -> p (b n)"), ACT.Copy).then_inc(pt1_done, 1)
                if v >= 2 and (v - 2) % 2 == 1:
                    u = (v - 2) // 2
                    b, hg = divmod(u, NG)
                    act.wait_ge(av_done, 2 * u + 2)
                    a.activation(osum[:, hg, b * S:(b + 1) * S], PS[:, 6 + u % 2, 0:S], ACT.Copy).then_inc(o_done, 1)


            act.wait_ge(lnT_done, 4)
            a.activation(attT[:, :, S:T], PS[:, 1, :].rearrange("p (k n) -> p k n", k=KD), ACT.Copy).then_inc(attT1_done, 1)
            act.wait_ge(lnT_done, 6)
            a.activation(xT[:, :, S:T], PS[:, 3, :].rearrange("p (k n) -> p k n", k=KD), ACT.Copy).then_inc(xT1_done, 1)

            for c in range(NC + 1):
                if c < NC:
                    act.wait_ge(xbias_done, c + 1)
                    if c >= 2:
                        act.wait_ge(xpT_done, c - 1)
                    a.activation(xp[c % 2], PS[:, 4 + c % 2, :], ACT.Exp, bias=xbias[:, c:c + 1], scale=D ** -0.5,
                                 accum_out=xsum[:, c:c + 1]).then_inc(xexp_done, 1)
                if c >= 1:
                    w = c - 1
                    act.wait_ge(xpT_done, w + 1)
                    if w >= 2:
                        act.wait_ge(xav_done, w - 1)
                    a.activation(xpt[w % 2].rearrange("p h q -> p (h q)"), PS[:, 6 + w % 2, :], ACT.Copy
                                 ).then_inc(xpt_done, 1)

            act.wait_ge(lnT_done, 8)
            a.activation(xT[:, :, S:T], PS[:, 3, :].rearrange("p (k n) -> p k n", k=KD), ACT.Copy).then_inc(xT1_done, 1)
            for j in range(2):
                act.wait_ge((xT0_done, xT1_done)[j], 3)
                a.activation(XH[:, :, j * S:(j + 1) * S], xT[:, :, j * S:(j + 1) * S], ACT.Copy).then_inc(xh_done, 1)
            act.wait_ge(dlog_done, 1)
            a.activation(elog[:, :, :], dlog[:, :, :], ACT.Exp).then_inc(elog_done, 1)

            def expert(e, slot, pair):
                for m in range(2):
                    act.wait_ge(gcl_done, e * 2 + (m + 1))
                    wait(act, glu_done, e * 2 + (m - 1))
                    a.activation(sig[:, m, :], gcl[:, m, :], ACT.Sigmoid, scale=ALPHA).then_inc(sig_done, 1)

                def high(m):
                    act.wait_ge(hid_done, e * 2 + (m + 1))
                    wait(act, y_done, (e - 1) * 2)
                    a.activation(HH[slot][:, m, :], hid[:, m, :], ACT.Copy).then_inc(hh_done, 1)

                high(0)
                if not isinstance(e, int) or e + 2 < E:
                    high_gate_up(e + 2, slot, pair + 1)
                high(1)
                if not isinstance(e, int) or e + 1 < E:
                    high_down(e + 1, 1 - slot, pair + slot)

            all_experts(act, expert)

        @block.vector
        def _(dve):
            v_ = nc.vector
            step = [0]

            def link(ins):
                step[0] += 1
                ins.then_inc(dve_step, 1)
                dve.wait_ge(dve_step, step[0])

            def row_stats(src, c):
                v_.bn_stats(stats[:, c, :], src[:, c, :]).then_inc(bn_done, 1)

            def normalise(src, n):
                dve.wait_ge(bn_done, (n + 1) * NC)
                for c in range(NC):
                    i = v_.bn_aggr(mv[:, c, :], stats[:, c, :])
                link(i)
                v_.tensor_scalar(ve[:, :], mv[:, :, 1], EPS, None, ALU.add).then_inc(stat_done, 1)
                dve.wait_ge(rstd_done, n + 1)
                for c in range(NC):
                    v_.tensor_scalar(xn[:, c, :], src[:, c, :], mv[:, c, 0:1], rstd[:, c:c + 1], ALU.subtract, ALU.mult
                                     ).then_inc(xn_done, 1)

            dve.wait_ge(x_in, 16)
            for c in range(NC):
                row_stats(x, c)
            normalise(x, 0)
            dve.wait_ge(lnT_done, 1)
            v_.tensor_copy(xT[:, :, 0:S], PS[:, 0, :].rearrange("p (k n) -> p k n", k=KD)).then_inc(xT0_done, 1)
            dve.wait_ge(param_in, 16)
            v_.tensor_scalar(bup1[:, :, :], gub[:, :, 1, :], 1.0, None, ALU.add)
            dve.wait_ge(mask_in, 16)
            link(v_.tensor_copy(maskf[:, :], mask8[:, :]))
            v_.tensor_scalar(pen[:, :], maskf[:, :], -1.0, -NEG, ALU.add, ALU.mult).then_inc(pen_done, 1)
            v_.tensor_reduce(valid1[:, :], maskf[:, :].rearrange("p (b m) -> p b m", b=B), AX.X, ALU.max).then_inc(pen_done, 1)
            for m in range(KD):
                dve.wait_ge(q_ps, m + 1)
                v_.tensor_scalar(qT[:, m, :], PS[:, 2 + m, :], bq[:, m:m + 1], DH ** -0.25, ALU.add, ALU.mult
                                 ).then_inc(q_done, 1)
            for m in range(KD):
                dve.wait_ge(k_ps, m + 1)
                v_.tensor_scalar(kT[:, m, :], PS[:, 4 + m, :], bk[:, m:m + 1], DH ** -0.25, ALU.add, ALU.mult
                                 ).then_inc(k_done, 1)
            for k in range(KD):
                dve.wait_ge(k_done, k + 1)
                dve.wait_ge(const_done, 1)
                for h in range(G8):
                    i = v_.tensor_scalar(kblk[:, k, h, :], kT[:, k, 0:S], headmask[:, h:h + 1], None, ALU.mult)
                i.then_inc(kblk_dve, 1)
            dve.wait_ge(row_in, 16)

            def take_values(b):
                for c in range(b * QC, (b + 1) * QC):
                    dve.wait_ge(v_ps, c // 2 * 2 + 2)
                    v_.tensor_tensor(vp[:, c, :, 0:DH], PS[:, 6 + c // 2, (c % 2) * D:(c % 2 + 1) * D].rearrange("p (h d) -> p h d", d=DH),
                                     bv_b.rearrange("p (h d) -> p h d", d=DH), ALU.add).then_inc(v_done, 1)

            take_values(0)
            NV = 2 * B * NG
            for v in range(NV + 4):
                if v < NV:
                    u = v // 2
                    if v >= 2:
                        dve.wait_ge(exp_done, v - 1)
                    if v % 2 == 0:
                        dve.wait_ge(sc_done, 3 * u + 1)
                        v_.tensor_reduce(nmax[:, 0, :], PS[:, 0, :].rearrange("p (h k) -> p h k", h=HG), AX.X, ALU.max,
                                         negate=True).then_inc(max_done, 1)
                    else:
                        for j in range(2):
                            dve.wait_ge(sc_done, 3 * u + 2 + j)
                            v_.tensor_reduce(nmax[:, 1, 2 * j:2 * j + 2], PS[:, 1 + j, :].rearrange("p (h k) -> p h k", h=2),
                                             AX.X, ALU.max, negate=True).then_inc(max_done, 1)
                if v == 1:
                    take_values(1)
                if 1 <= v <= NV and (v - 1) % 2 == 0:
                    w = v - 1
                    dve.wait_ge(pT_done, w + 1)
                    if w >= 2:
                        dve.wait_ge(av_done, w - 1)
                    v_.tensor_copy(pt0[:, :, :].rearrange("p h q -> p (h q)"), PS[:, 3, :]).then_inc(pt0_done, 1)
                if v >= 5 and (v - 5) % (2 * NG) == 2 * NG - 2:
                    b = (v - 5) // (2 * NG)
                    dve.wait_ge(back_done, b + 1)
                    heads = PS[:, 4:6, :].rearrange("p c (h i) -> p c h i", i=HP)
                    link(v_.reciprocal(rsum[:, :, :], heads[:, :, :, DH]))
                    for qc in range(QC):
                        v_.tensor_tensor(att[:, b * QC + qc, :].rearrange("p (h i) -> p h i", i=DH), heads[:, qc, :, 0:DH],
                                         rsum[:, qc, :].unsqueeze(2).to_broadcast([P, H, DH]), ALU.mult).then_inc(att_done, 1)
            dve.wait_ge(lnT_done, 3)
            v_.tensor_copy(attT[:, :, 0:S], PS[:, 0, :].rearrange("p (k n) -> p k n", k=KD)).then_inc(attT0_done, 1)
            dve.wait_ge(const_done, 1)
            for c in range(NC):
                dve.wait_ge(proj_done, c + 1)
                link(v_.tensor_tensor(x2[:, c, :], PS[:, (4, 5, 2, 3)[c], 0:D], xb[:, c, :], ALU.add))
                row_stats(x2, c)
            normalise(x2, 1)
            dve.wait_ge(lnT_done, 5)
            v_.tensor_copy(xT[:, :, 0:S], PS[:, 2, :].rearrange("p (k n) -> p k n", k=KD)).then_inc(xT0_done, 1)
            dve.wait_ge(valid_ps, 1)
            v_.tensor_copy(valid[:, :], PS[:, 0, 0:B]).then_inc(valid_done, 1)
            dve.wait_ge(valid_done, 1)
            for c in range(NC + 2):
                if c < NC:
                    dve.wait_ge(xs_done, c + 1)
                    link(v_.tensor_reduce(xmax[:, c:c + 1], PS[:, 4 + c % 2, :], AX.X, ALU.max))
                    v_.tensor_scalar(xbias[:, c:c + 1], xmax[:, c:c + 1], -(D ** -0.5), None, ALU.mult
                                     ).then_inc(xbias_done, 1)
                if c >= 2:
                    w = c - 2
                    dve.wait_ge(xexp_done, w + 1)
                    link(v_.reciprocal(xrec[:, w:w + 1], xsum[:, w:w + 1]))
                    link(v_.tensor_tensor(xrv[:, w:w + 1], xrec[:, w:w + 1], valid[:, w // QC:w // QC + 1], ALU.mult))
                    dve.wait_ge(xav_done, w + 1)
                    v_.scalar_tensor_tensor(out=x3[:, w, :], in0=PS[:, w % 2, 0:D], scalar=xrv[:, w:w + 1],
                                            in1=x2[:, w, :], op0=ALU.mult, op1=ALU.add).then_inc(x3_done, 1)
                    dve.wait_ge(x3_done, w + 1)
                    row_stats(x3, w)
            normalise(x3, 2)
            dve.wait_ge(lnT_done, 7)
            v_.tensor_copy(xT[:, :, 0:S], PS[:, 2, :].rearrange("p (k n) -> p k n", k=KD)).then_inc(xT0_done, 1)
            for j in range(2):
                dve.wait_ge(xh_done, j + 1)
                half_ = slice(j * S, (j + 1) * S)
                v_.tensor_tensor(XL[:, :, half_], xT[:, :, half_], XH[:, :, half_].bitcast(F32), ALU.subtract).then_inc(xl_done, 1)

            dve.wait_ge(logit_ps, 1)
            link(v_.tensor_tensor(logits[:, :, :], PS[:, 4, 0:NC * E].rearrange("p (c e) -> p c e", e=E),
                                  rb_b.unsqueeze(1).to_broadcast([P, NC, E]), ALU.add))
            for c in range(NC):
                i = v_.max(top8[:, c, :], logits[:, c, :])
            link(i)
            kth = top8[:, :, TOP_K - 1:TOP_K].to_broadcast([P, NC, E])
            v_.tensor_tensor(dlog[:, :, :], logits[:, :, :], top8[:, :, 0:1].to_broadcast([P, NC, E]), ALU.subtract
                             ).then_inc(dlog_done, 1)
            v_.tensor_tensor(gt[:, :, :], logits[:, :, :], kth, ALU.is_gt)
            link(v_.tensor_tensor(eq[:, :, :], logits[:, :, :], kth, ALU.is_equal))
            link(v_.tensor_reduce(cnt[:, :], gt[:, :, :], AX.X, ALU.add))
            v_.tensor_scalar(need[:, :], cnt[:, :], -1.0, float(TOP_K), ALU.mult, ALU.add)
            for c in range(NC):
                i = v_.tensor_tensor_scan(rank[:, c, :], ones_f[:, :], eq[:, c, :], 0.0, ALU.mult, ALU.add)
            link(i)
            link(v_.tensor_tensor(within[:, :, :], rank[:, :, :], need[:, :].unsqueeze(2).to_broadcast([P, NC, E]), ALU.is_le))
            link(v_.tensor_tensor(sel_eq[:, :, :], eq[:, :, :], within[:, :, :], ALU.mult))
            link(v_.tensor_tensor(sel[:, :, :], sel_eq[:, :, :], gt[:, :, :], ALU.add))
            dve.wait_ge(elog_done, 1)
            link(v_.tensor_tensor(esel[:, :, :], elog[:, :, :], sel[:, :, :], ALU.mult))
            link(v_.tensor_reduce(etot[:, :], esel[:, :, :], AX.X, ALU.add))
            link(v_.reciprocal(erec[:, :], etot[:, :]))
            v_.tensor_tensor(score[:, :, :], esel[:, :, :], erec[:, :].unsqueeze(2).to_broadcast([P, NC, E]), ALU.mult
                             ).then_inc(score_done, 1)

            dve.wait_ge(scoreT_ps, 1)
            v_.tensor_copy(scoreT[:, :], PS[0:E, 5, :]).then_inc(scoreT_done, 1)

            def weighted_sum(e, slot, chunks):
                for c in chunks:
                    if c % 2 == 0:
                        dve.wait_ge(y_done, e * 2 + (c // 2 + 1))
                    dve.wait_ge(acc_done, e * NC + (c + 1))
                    v_.scalar_tensor_tensor(out=acc[:, c, :], in0=PS[:, 4 + 2 * slot + c // 2, (c % 2) * D:(c % 2 + 1) * D],
                                            scalar=score[:, c, bass.ds(e, 1)], in1=acc[:, c, :], op0=ALU.mult, op1=ALU.add
                                            ).then_inc(acc_done, 1)

            def expert(e, slot, pair):
                def clamp_gate(m):
                    dve.wait_ge(gu_done, e * 4 + (2 * m + 1))
                    wait(dve, glu_done, e * 2 + (m - 1))
                    v_.tensor_scalar(gcl[:, m, :], PS[:, 2 * m, :], gub[:, bass.ds(e, 1), 0, m], LIMIT, ALU.add, ALU.min
                                     ).then_inc(gcl_done, 1)

                def clamp_up(m):
                    dve.wait_ge(gu_done, e * 4 + (2 * m + 2))
                    wait(dve, hid_done, e * 2 + (m - 1))
                    v_.tensor_scalar(upc[:, m, :], PS[:, 2 * m + 1, :], bup1[:, bass.ds(e, 1), m], 1.0 - LIMIT, ALU.add, ALU.max
                                     ).then_inc(upc_done, 1)

                def product(m):
                    dve.wait_ge(glu_done, e * 2 + (m + 1))
                    dve.wait_ge(upc_done, e * 2 + (m + 1))
                    wait(dve, hl_done, e * 2 + (m - 1))
                    v_.scalar_tensor_tensor(out=hid[:, m, :], in0=upc[:, m, :], scalar=1.0 + LIMIT, in1=glu[:, m, :],
                                            op0=ALU.min, op1=ALU.mult).then_inc(hid_done, 1)

                def low(m):
                    dve.wait_ge(hh_done, e * 2 + (m + 1))
                    v_.tensor_tensor(HL[slot][:, m, :], hid[:, m, :], HH[slot][:, m, :].bitcast(F32), ALU.subtract
                                     ).then_inc(hl_done, 1)

                clamp_gate(0)
                clamp_up(0)
                clamp_gate(1)
                product(0)
                clamp_up(1)
                low(0)
                product(1)
                if isinstance(e, int) and e == 0:
                    low(1)
                    for c in range(NC):
                        dve.wait_ge(dbias_ps, c // 2 * 2 + 2)
                        v_.tensor_tensor(acc[:, c, :], PS[:, 6 + c // 2, (c % 2) * D:(c % 2 + 1) * D], x3[:, c, :], ALU.add
                                         ).then_inc(acc_done, 1)
                else:
                    weighted_sum(e - 1, 1 - slot, (0, 1))
                    low(1)
                    weighted_sum(e - 1, 1 - slot, (2, 3))

            all_experts(dve, expert)
            weighted_sum(E - 1, (E - 1) % 2, range(NC))

        @block.tensor
        def _(pe):
            t = nc.tensor

            def transposes(src, bank, ready=None, n=0):
                for c in range(NC):
                    if ready is not None:
                        pe.wait_ge(ready, n * NC + c + 1)
                    for k in range(KD):
                        i = t.transpose(PS[:, bank + c // 2, (k * 2 + c % 2) * P:(k * 2 + c % 2 + 1) * P],
                                        src[:, c, k * P:(k + 1) * P], ident[:, :])
                    if c % 2 == 1:
                        i.then_inc(lnT_done, 1)

            pe.wait_ge(warm_done, 1)
            for _ in range(16):
                t.matmul(PS[:, 7, :], warm[:, 0:P], warm[:, :], start=True, stop=True)
            pe.wait_ge(ident_done, 1)
            transposes(xn, 0, xn_done, 0)
            pe.wait_ge(qkv_in, 16)
            pe.wait_ge(xT0_done, 1)
            pe.wait_ge(xT1_done, 1)
            for j, (bank, done) in enumerate(((2, q_ps), (4, k_ps))):
                for m in range(KD):
                    for k in range(KD):
                        i = t.matmul(PS[:, bank + m, :], wqkv[:, j, k, m * P:(m + 1) * P], xT[:, k, :], start=(k == 0), stop=(k == KD - 1))
                    i.then_inc(done, 1)

            def project_values(b):
                for c in range(b * QC, (b + 1) * QC):
                    for k in range(KD):
                        i = t.matmul(PS[:, 6 + c // 2, (c % 2) * D:(c % 2 + 1) * D], xT[:, k, c * P:(c + 1) * P], wqkv[:, 2, k, :],
                                     start=(k == 0), stop=(k == KD - 1))
                    i.then_inc(v_ps, 1)

            project_values(0)

            NV = 2 * B * NG
            pe.wait_ge(q_done, KD)

            def scores(v):
                u, qc = divmod(v, 2)
                b, hg = divmod(u, NG)
                g, h0 = hg // 2, (hg % 2) * HG
                if b == 0:
                    pe.wait_ge(kblk_dve, g + 1)
                else:
                    pe.wait_ge(kblk_pool, g + 1)
                if v >= 2:
                    pe.wait_ge(exp_done, v - 1)
                q = qT[:, g, b * S + qc * P:b * S + (qc + 1) * P]
                keys = kblk[:, b * KD + g]
                if qc == 0:
                    out = PS[:, 0, :].rearrange("p (h k) -> p h k", h=HG)
                    t.matmul(out, q, keys[:, h0:h0 + HG, 0:P], start=True, stop=False)
                    t.matmul(out, ident_bf[:, :], causal[:, :].unsqueeze(1).to_broadcast([P, HG, P]), start=False, stop=True
                             ).then_inc(sc_done, 1)
                else:
                    for j in range(2):
                        out = PS[:, 1 + j, :].rearrange("p (h k) -> p h k", h=2)
                        t.matmul(out, q, keys[:, h0 + 2 * j:h0 + 2 * j + 2, :], start=True, stop=False)
                        t.matmul(out[:, :, P:S], ident_bf[:, :], causal[:, :].unsqueeze(1).to_broadcast([P, 2, P]),
                                 start=False, stop=True).then_inc(sc_done, 1)

            def turn(v):
                pe.wait_ge(exp_done, v + 1)
                if v % 2 == 0:
                    if v >= 2:
                        pe.wait_ge(pt0_done, v // 2)
                    for h in range(HG):
                        i = t.transpose(PS[:, 3, h * P:(h + 1) * P], pr0[:, h, :], ident[:, :])
                else:
                    if v >= 2:
                        pe.wait_ge(pt1_done, v // 2)
                    if v > 2 * NG + 2:
                        pe.wait_ge(att_done, QC)
                    for kc in range(QC):
                        for h in range(HG):
                            i = t.transpose(PS[:, 4 + kc, h * P:(h + 1) * P], pr1[:, h, kc * P:(kc + 1) * P], ident[:, :])
                i.then_inc(pT_done, 1)

            def values(v):
                u, qc = divmod(v, 2)
                b, hg = divmod(u, NG)
                if v % (2 * NG) == 0:
                    pe.wait_ge(v_done, QC * (b + 1))
                if qc == 0:
                    pe.wait_ge(pt0_done, u + 1)
                    if u == 1:
                        pe.wait_ge(v_done, NC)
                    if u >= 2:
                        pe.wait_ge(o_done, u - 1)
                else:
                    pe.wait_ge(pt1_done, u + 1)
                for kc in range(qc + 1):
                    for h in range(HG):
                        p = pt0[:, h, :] if qc == 0 else pt1[:, kc, h, :]
                        i = t.matmul(PS[HP * h:HP * (h + 1), 6 + u % 2, qc * P:(qc + 1) * P], vp[:, b * QC + kc, hg * HG + h, :], p,
                                     start=(kc == 0), stop=(kc == qc))
                i.then_inc(av_done, 1)

            def turn_back(b):
                u = (b + 1) * NG - 1
                pe.wait_ge(o_done, u + 1)
                pe.wait_ge(pt1_done, min(u + 2, B * NG))
                for qc in range(QC):
                    for hg in range(NG):
                        i = t.transpose(PS[:, 4 + qc, hg * P:(hg + 1) * P], osum[:, hg, b * S + qc * P:b * S + (qc + 1) * P], ident[:, :])
                i.then_inc(back_done, 1)

            for v in range(NV + 4):
                if v < NV:
                    scores(v)
                if v == 1:
                    project_values(1)
                if 1 <= v <= NV:
                    turn(v - 1)
                if 2 <= v <= NV + 1:
                    values(v - 2)
                if v >= 5 and (v - 5) % (2 * NG) == 2 * NG - 2:
                    turn_back((v - 5) // (2 * NG))

            pe.wait_ge(att_done, NC)
            transposes(att, 0)
            pe.wait_ge(wo_in, 16)
            for c in range(NC):
                if c % 2 == 0:
                    pe.wait_ge((attT0_done, attT1_done)[c // 2], 1)
                for k in range(KD):
                    i = t.matmul(PS[:, (4, 5, 2, 3)[c], 0:D], attT[:, k, c * P:(c + 1) * P], wo[:, k, :], start=(k == 0), stop=(k == KD - 1))
                i.then_inc(proj_done, 1)

            transposes(xn, 2, xn_done, 1)
            pe.wait_ge(pen_done, 2)
            pe.wait_ge(ctxT_in, 16)
            t.matmul(PS[:, 0, 0:B], one1[:, :], valid1[:, :], start=True, stop=True).then_inc(valid_ps, 1)
            for c in range(NC + 2):
                if c < NC:
                    if c % 2 == 0:
                        pe.wait_ge((xT0_done, xT1_done)[c // 2], 2)
                    if c >= 2:
                        pe.wait_ge(xexp_done, c - 1)
                    b = c // QC
                    for k in range(KD):
                        t.matmul(PS[:, 4 + c % 2, :], xT[:, k, c * P:(c + 1) * P], ctxT[:, b * KD + k, :], start=(k == 0), stop=False)
                    t.matmul(PS[:, 4 + c % 2, :], ones_bf[:, :], pen[:, b * M:(b + 1) * M], start=False, stop=True
                             ).then_inc(xs_done, 1)
                if 1 <= c <= NC:
                    w = c - 1
                    pe.wait_ge(xexp_done, w + 1)
                    if w >= 2:
                        pe.wait_ge(xpt_done, w - 1)
                    for j in range(KM):
                        i = t.transpose(PS[:, 6 + w % 2, j * P:(j + 1) * P], xp[w % 2][:, j * P:(j + 1) * P], ident[:, :])
                    i.then_inc(xpT_done, 1)
                if c >= 2:
                    w = c - 2
                    pe.wait_ge(xpt_done, w + 1)
                    if w == 0:
                        pe.wait_ge(ctx_in, 16)
                        pe.wait_ge(valid_done, 1)
                    if w >= 2:
                        pe.wait_ge(x3_done, w - 1)
                    for j in range(KM):
                        i = t.matmul(PS[:, w % 2, 0:D], xpt[w % 2][:, j, :], ctx_sb[:, (w // QC) * KM + j, :], start=(j == 0), stop=(j == KM - 1))
                    i.then_inc(xav_done, 1)

            transposes(xn, 2, xn_done, 2)
            pe.wait_ge(xT0_done, 3)
            pe.wait_ge(xT1_done, 3)
            for c in range(NC):
                for k in range(KD):
                    i = t.matmul(PS[:, 4, c * E:(c + 1) * E], xT[:, k, c * P:(c + 1) * P], routerT[:, k, :], start=(k == 0), stop=(k == KD - 1))
            i.then_inc(logit_ps, 1)

            def gate_up(e, slot):
                pe.wait_ge(wlg_done, e + 1)
                for m in range(2):
                    for part in range(2):
                        wait(pe, gcl_done if part == 0 else upc_done, e * 2 + (m - 1))
                        n = 0
                        for k in range(KD):
                            for w, xx in ((WHg, XH), (WHg, XL), (WLg, XH)):
                                i = t.matmul(PS[:, 2 * m + part, :], w[slot][:, k, part, m * P:(m + 1) * P], xx[:, k, :],
                                             start=(n == 0), stop=(n == 3 * KD - 1))
                                n += 1
                        i.then_inc(gu_done, 1)

            def down(e, slot):
                pe.wait_ge(hl_done, e * 2 + 2)
                pe.wait_ge(wld_done, e + 1)
                wait(pe, acc_done, (e - 1) * NC)
                for c in range(NC):
                    n = 0
                    for k in range(KD):
                        for hh, w in ((HH, WHd), (HL, WHd), (HH, WLd)):
                            i = t.matmul(PS[:, 4 + 2 * slot + c // 2, (c % 2) * D:(c % 2 + 1) * D], hh[slot][:, k, c * P:(c + 1) * P],
                                         w[slot][:, k, :], start=(n == 0), stop=(n == 3 * KD - 1))
                            n += 1
                    if c % 2 == 1:
                        i.then_inc(y_done, 1)

            pe.wait_ge(xl_done, KD)
            gate_up(0, 0)
            pe.wait_ge(score_done, 1)
            for c in range(NC):
                i = t.transpose(PS[0:E, 5, c * P:(c + 1) * P], score[:, c, :], ident[:, :])
            i.then_inc(scoreT_ps, 1)
            def weighted_biases():
                pe.wait_ge(scoreT_done, 1)
                pe.wait_ge(dbias_in, 16)
                for c in range(NC):
                    t.matmul(PS[:, 6 + c // 2, (c % 2) * D:(c % 2 + 1) * D], scoreT[:, c * P:(c + 1) * P], dbias[:, :], start=True, stop=True
                             ).then_inc(dbias_ps, 1)

            def both(e, slot, pair):
                if not isinstance(e, int) or e + 1 < E:
                    gate_up(e + 1, 1 - slot)
                if isinstance(e, int) and e == 0:
                    weighted_biases()
                down(e, slot)

            all_experts(pe, both)


def kernel(**inputs):
    import numpy as np
    import concourse.bacc as bacc
    from concourse.bass_utils import run_bass_kernel_spmd

    a = {n: np.ascontiguousarray(v) for n, v in inputs.items()}

    def rows_in(w):
        return w.reshape(-1, P, w.shape[-1]).transpose(1, 0, 2)

    wqkv = np.stack([rows_in(a[f"L0_attn_W{n}"].T) for n in "qkv"], axis=1)
    wo = rows_in(a["L0_attn_Wo"].T)
    gub = a["L0_ffn_gate_up_proj_bias"].reshape(E, KD, P, 2).transpose(2, 0, 3, 1)
    params = np.concatenate([a["L0_attn_bq"].reshape(KD, P).T, a["L0_attn_bk"].reshape(KD, P).T, gub.reshape(P, -1),
                             rows_in(a["L0_ffn_router_weight"].T).reshape(P, -1)], axis=1)
    rows = np.concatenate([a["L0_attn_bv"], a["L0_attn_bo"], a["L0_ffn_router_bias"]])
    gup = a["L0_ffn_gate_up_proj"].reshape(E, KD, P, F, 2).transpose(0, 2, 1, 4, 3).reshape(E, P, GU)
    down = a["L0_ffn_down_proj"].reshape(E, KD, P, D).transpose(0, 2, 1, 3).reshape(E, P, DW)
    ctxT = a["ctx_2048"].transpose(2, 0, 1).reshape(KD, P, B, M).transpose(1, 2, 0, 3).reshape(P, B * KD, M)
    arrays = {
        "x_d": a["x"], "ctx_d": a["ctx_2048"], "ctxT_d": ctxT, "wqkv_d": wqkv, "wo_d": wo, "params_d": params,
        "rows_d": rows, "mask_d": a["mask_BxS2_bk0"].reshape(-1), "dbias_d": a["L0_ffn_down_proj_bias"],
        "we_d": np.concatenate([gup, down], axis=2),
    }
    arrays = {n: np.ascontiguousarray(v) for n, v in arrays.items()}
    nc = bacc.Bacc("TRN2", target_bir_lowering=False, num_devices=1)
    args = [nc.dram_tensor(n, v.shape, mybir.dt.from_np(v.dtype), kind="ExternalInput").ap() for n, v in arrays.items()]
    out = nc.dram_tensor("out_d", (B, S, D), F32, kind="ExternalOutput").ap()
    decoder_layer(nc, *args, out)
    got = run_bass_kernel_spmd(nc, [arrays], core_ids=[0])
    return got.results[0]["out_d"]
```

```python
from contextlib import ExitStack

import concourse.bass as bass
from concourse import mybir

F32 = mybir.dt.float32
F32R = mybir.dt.float32r
BF16 = mybir.dt.bfloat16
U8 = mybir.dt.uint8
ALU = mybir.AluOpType
ACT = mybir.ActivationFunctionType
AX = mybir.AxisListType

P = 128
B, S, D = 2, 256, 256
M = 512
H, DH = 16, 16
E, F = 16, 256
TOP_K = 4
T = B * S
NC = T // P
QC = S // P
KD = D // P
KM = M // P
HG = 4
NG = H // HG
G8 = P // DH
BLK = 3
HP = 32
EPS = 1e-5
ALPHA, LIMIT = 1.702, 7.0
NEG = -1e30
GU = 2 * F * KD
DW = D * KD


def decoder_layer(nc, x_d, ctx_d, ctxT_d, wqkv_d, wo_d, params_d, rows_d, mask_d, dbias_d, we_d, out_d):
    ctx = ExitStack()
    with ctx:
        def sb(name, shape, dt=F32):
            return ctx.enter_context(nc.sbuf_tensor(name, shape, dt))

        def sem(name):
            return ctx.enter_context(nc.semaphore(name))

        PS = ctx.enter_context(nc.psum_tensor("PS", [P, 8, 512], F32))

        x = sb("x", [P, NC, D])
        ctx_sb = sb("ctx_sb", [P, B * KM, D])
        ctxT = sb("ctxT", [P, B * KD, M])
        wqkv = sb("wqkv", [P, 3, KD, D])
        wo = sb("wo", [P, KD, D])
        params = sb("params", [P, 4 + 4 * E + KD * E])
        rows = sb("rows", [P, 2 * D + E])
        mask8 = sb("mask8", [1, B * M], U8)
        dbias = sb("dbias", [E, D])
        raw_g = [sb(f"raw_g{i}", [P, GU]) for i in range(2)]
        raw_w = [sb(f"raw_w{i}", [P, DW]) for i in range(2)]
        bq, bk = params[:, 0:2], params[:, 2:4]
        gub = params[:, 4:4 + 4 * E].rearrange("p (e g m) -> p e g m", e=E, g=2)
        routerT = params[:, 4 + 4 * E:].rearrange("p (k e) -> p k e", k=KD)
        bv_b, bo_b, rb_b = rows[:, 0:D], rows[:, D:2 * D], rows[:, 2 * D:]

        ident = sb("ident", [P, P])
        ident_bf = sb("ident_bf", [P, P], BF16)
        causal = sb("causal", [P, P], BF16)
        headmask = sb("headmask", [P, G8])
        parity = sb("parity", [P, 2])
        ones_bf = sb("ones_bf", [1, P], BF16)
        warm = sb("warm", [P, 512], BF16)
        half = sb("half", [P, NC])
        ones_f = sb("ones_f", [P, E])
        one1 = sb("one1", [1, P])

        xb = sb("xb", [P, NC, D])
        xn = sb("xn", [P, NC, D])
        xT = sb("xT", [P, KD, T])
        qT = sb("qT", [P, KD, T])
        kpar = sb("kpar", [P, KD, 2, T])
        vp = sb("vp", [P, NC, H, HP])
        pr = sb("pr", [P, 2, 2, BLK * P])
        pt = sb("pt", [P, 2, HG, BLK, P])
        nmax = sb("nmax", [P, 2, 2, QC])
        osum = sb("osum", [P, NG, T])
        rsum = sb("rsum", [P, QC, H])
        att = sb("att", [P, NC, D])
        attT = sb("attT", [P, KD, T])
        x2 = sb("x2", [P, NC, D])
        x3 = sb("x3", [P, NC, D])
        stats = sb("stats", [P, NC, 6])
        mv = sb("mv", [P, NC, 2])
        ve = sb("ve", [P, NC])
        rstd = sb("rstd", [P, NC])
        maskf = sb("maskf", [1, B * M])
        pen = sb("pen", [1, B * M], BF16)
        valid1 = sb("valid1", [1, B])
        valid = sb("valid", [P, B])
        xmax = sb("xmax", [P, NC])
        xscale = sb("xscale", [P, NC])
        xbias = sb("xbias", [P, NC])
        xsum = sb("xsum", [P, NC])
        xrec = sb("xrec", [P, NC])
        xrv = sb("xrv", [P, NC])
        logits = sb("logits", [P, NC, E])
        top8 = sb("top8", [P, NC, 8])
        gt = sb("gt", [P, NC, E])
        eq = sb("eq", [P, NC, E])
        rank = sb("rank", [P, NC, E])
        need = sb("need", [P, NC])
        cnt = sb("cnt", [P, NC])
        within = sb("within", [P, NC, E])
        sel_eq = sb("sel_eq", [P, NC, E])
        sel = sb("sel", [P, NC, E])
        dlog = sb("dlog", [P, NC, E])
        elog = sb("elog", [P, NC, E])
        esel = sb("esel", [P, NC, E])
        etot = sb("etot", [P, NC])
        erec = sb("erec", [P, NC])
        score = sb("score", [P, NC, E])
        scoreT = sb("scoreT", [E, T])

        XH = sb("XH", [P, KD, T], F32R)
        XL = sb("XL", [P, KD, T], F32R)
        WHg = [sb(f"WHg{i}", [P, KD, 2, F], F32R) for i in range(2)]
        WLg = [sb(f"WLg{i}", [P, KD, 2, F], F32R) for i in range(2)]
        WHd = [sb(f"WHd{i}", [P, KD, D], F32R) for i in range(2)]
        WLd = [sb(f"WLd{i}", [P, KD, D], F32R) for i in range(2)]
        HH = [sb(f"HH{i}", [P, KD, T], F32R) for i in range(2)]
        HL = [sb(f"HL{i}", [P, KD, T], F32R) for i in range(2)]
        bup1 = sb("bup1", [P, E, 2])
        kh = [HH[m][:, :, :].rearrange("p k t -> p (k t)").rearrange("p (r t) -> p r t", r=2) for m in range(KD)]
        kl = [HL[m][:, :, :].rearrange("p k t -> p (k t)").rearrange("p (r t) -> p r t", r=2) for m in range(KD)]
        qh, ql = ([X[:, m, 0:B * P].rearrange("p (b q) -> p b q", b=B) for m in range(KD)] for X in (XH, XL))
        q2 = [qT[:, m, :].rearrange("p (b c q) -> p b c q", b=B, c=QC)[:, :, QC - 1, :] for m in range(KD)]
        keys_flat = kpar[:, :, :, :].rearrange("p k r t -> p (k r t)")
        pt_flat = pt[:, :, :, :, :].rearrange("p s h c q -> p (s h c q)")
        xp = [keys_flat[:, i * M:(i + 1) * M] for i in range(2)]
        xpt = [keys_flat[:, (2 + i) * M:(3 + i) * M].rearrange("p (c q) -> p c q", q=P) for i in range(2)]
        gcl, sig = (keys_flat[:, i * KD * T:(i + 1) * KD * T].rearrange("p (m t) -> p m t", m=KD) for i in range(2))
        glu, upc, hid = (pt_flat[:, i * KD * T:(i + 1) * KD * T].rearrange("p (m t) -> p m t", m=KD) for i in range(3))
        acc = x3

        qkv_in = [sem(f"w{n}_in") for n in "qkv"]
        x_in = [sem(f"x_in{c}") for c in range(NC)]
        param_in, row_in, ctx_in, ctxT_in, wo_in, mask_in, dbias_in = (
            sem(n) for n in ("param_in", "row_in", "ctx_in", "ctxT_in", "wo_in", "mask_in", "dbias_in"))
        raw_g_in = [sem(f"raw_g_in{i}") for i in range(2)]
        raw_w_in = [sem(f"raw_w_in{i}") for i in range(2)]
        const_step, xb_done, ident_done, warm_done = (sem(n) for n in ("const_step", "xb_done", "ident_done", "warm_done"))
        dve_step = sem("dve_step")
        bn_done, stat_done, rstd_done, xn_done = sem("bn_done"), sem("stat_done"), sem("rstd_done"), sem("xn_done")
        lnT_done = sem("lnT_done")
        xT_done = [sem(f"xT_done{b}") for b in range(B)]
        attT_done = [sem(f"attT_done{b}") for b in range(B)]
        q_ps, k_ps, v_ps = sem("q_ps"), sem("k_ps"), sem("v_ps")
        q_done, k_done, v_done = sem("q_done"), sem("k_done"), sem("v_done")
        parity_done, mask_done = sem("parity_done"), sem("mask_done")
        sc_done, max_done, exp_done, pT_done = sem("sc_done"), sem("max_done"), sem("exp_done"), sem("pT_done")
        pt_done = [sem(f"pt_done{j}") for j in range(2)]
        av_done, o_done = sem("av_done"), sem("o_done")
        back_done, att_done, proj_done = (sem(n) for n in ("back_done", "att_done", "proj_done"))
        pen_done, valid_ps, valid_done = sem("pen_done"), sem("valid_ps"), sem("valid_done")
        xs_done, xbias_done, xexp_done, xpT_done = sem("xs_done"), sem("xbias_done"), sem("xexp_done"), sem("xpT_done")
        xpt_done, xav_done, x3_done = sem("xpt_done"), sem("xav_done"), sem("x3_done")
        xh_done, xl_done = sem("xh_done"), sem("xl_done")
        kh_done, kl_done, qh_done, ql_done = (sem(n) for n in ("kh_done", "kl_done", "qh_done", "ql_done"))
        logit_ps, dlog_done, elog_done, score_done = sem("logit_ps"), sem("dlog_done"), sem("elog_done"), sem("score_done")
        scoreT_ps, scoreT_done, dbias_ps = sem("scoreT_ps"), sem("scoreT_done"), sem("dbias_ps")
        whg_done, wlg_done, whd_done, wld_done = sem("whg_done"), sem("wlg_done"), sem("whd_done"), sem("wld_done")
        gu_done, gcl_done, upc_done, sig_done, glu_done = (
            sem(n) for n in ("gu_done", "gcl_done", "upc_done", "sig_done", "glu_done"))
        hid_done, hh_done, hl_done, y_done, acc_done = (
            sem(n) for n in ("hid_done", "hh_done", "hl_done", "y_done", "acc_done"))
        scaled_done, added_done = sem("scaled_done"), sem("added_done")
        out_done = sem("out_done")

        XS_BANK, XT_BANK, XV_BANK = (7, 2, 4, 5), (3, 4, 6, 3), (1, 2, 4, 5)
        NV = 2 * B * NG
        TAIL = 2 * NG + 3

        block = ctx.enter_context(nc.Block())

        def wait(eng, s, value):
            if not isinstance(value, int) or value > 0:
                eng.wait_ge(s, value)

        LAST = E - 1
        LAST_BANK = (6, 6, 7, 0)
        PARTS = [(b, m) for b in range(B) for m in range(KD)]

        def all_experts(eng, body, last):
            for e in (0, 1):
                body(e, e, 0)
            with eng.Fori(1, E // 2 - 1) as pair:
                for slot in (0, 1):
                    body(pair * 2 + slot, slot, pair)
            body(LAST - 1, 0, LAST // 2)
            last()

        xv = x_d.rearrange("b (c p) d -> p (b c) d", p=P)
        ov = out_d.rearrange("b (c p) d -> p (b c) d", p=P)

        @block.sync
        def _(sp):
            for c in (0, 2):
                sp.dma_start(x[:, c, :], xv[:, c, :]).then_inc(x_in[c], 16)
            for j in (1, 0, 2):
                sp.dma_start(wqkv[:, j], wqkv_d[:, j]).then_inc(qkv_in[j], 16)
            for e in range(2):
                sp.dma_start(raw_g[e][:, :], we_d[e, :, 0:GU]).then_inc(raw_g_in[e], 16)
                sp.dma_start(raw_w[e][:, :], we_d[e, :, GU:]).then_inc(raw_w_in[e], 16)
            sp.dma_start(wo[:, :, :], wo_d).then_inc(wo_in, 16)
            sp.dma_start(ctxT[:, :, :], ctxT_d).then_inc(ctxT_in, 16)
            sp.dma_start(ctx_sb[:, :, :], ctx_d.rearrange("b (c p) d -> p (b c) d", p=P)).then_inc(ctx_in, 16)
            with sp.Fori(1, E // 2) as pair:
                for slot in (0, 1):
                    sp.wait_ge(wlg_done, pair * 2 + slot - 1)
                    expert = we_d[bass.ts(pair * 2 + slot, 1)].rearrange("e p n -> p (e n)")
                    sp.dma_start(raw_g[slot][:, :], expert[:, 0:GU]).then_inc(raw_g_in[slot], 16)
                    sp.wait_ge(wld_done, pair * 2 + slot - 1)
                    sp.dma_start(raw_w[slot][:, :], expert[:, GU:]).then_inc(raw_w_in[slot], 16)
            for c in range(NC):
                sp.wait_ge(acc_done, NC * LAST + c + 1)
                sp.dma_start(ov[:, c, :], acc[:, c, :]).then_inc(out_done, 16)
            sp.wait_ge(out_done, 16 * NC)

        @block.gpsimd
        def _(pool):
            step = [0]

            def link(ins):
                step[0] += 1
                ins.then_inc(const_step, 1)
                pool.wait_ge(const_step, step[0])

            g = nc.gpsimd
            g.memset(warm[:, :], 0.0).then_inc(warm_done, 1)
            g.memset(half[:, :], -0.5)
            link(g.memset(ident[:, :], 0.0))
            g.affine_select(out=ident[:, :], in_=ident[:, :], compare_op=ALU.not_equal, fill=1.0, base=0,
                            pattern=[[-1, P]], channel_multiplier=1).then_inc(ident_done, 1)
            link(g.memset(causal[:, :], 0.0))
            link(g.affine_select(out=causal[:, :], in_=causal[:, :], compare_op=ALU.is_ge, fill=NEG, base=0,
                                 pattern=[[-1, P]], channel_multiplier=1))
            pool.wait_ge(ident_done, 1)
            g.tensor_copy(ident_bf[:, :], ident[:, :])
            link(g.memset(headmask[:, :], DH ** -0.25))
            link(g.affine_select(out=headmask[:, :], in_=headmask[:, :], compare_op=ALU.is_ge, fill=0.0, base=0,
                                 pattern=[[-DH, G8]], channel_multiplier=1))
            g.affine_select(out=headmask[:, :], in_=headmask[:, :], compare_op=ALU.is_ge, fill=0.0, base=DH - 1,
                            pattern=[[DH, G8]], channel_multiplier=-1).then_inc(mask_done, 1)
            g.memset(ones_bf[:, :], 1.0)
            g.memset(ones_f[:, :], 1.0)
            g.memset(one1[:, :], 1.0)
            g.memset(vp[:, :, :, DH:HP], 1.0)

            def rstds(n):
                chunks = slice(0, NC) if n == 0 else slice((n - 1) % B * QC, (n - 1) % B * QC + QC)
                pool.wait_ge(stat_done, n + 1)
                g.tensor_tensor(rstd[:, chunks], ve[:, chunks], half[:, chunks], ALU.pow).then_inc(rstd_done, 1)

            rstds(0)
            pool.wait_ge(row_in, 16)
            for c in range(NC):
                pool.wait_ge(x_in[c], 16)
                i = g.tensor_tensor(xb[:, c, :], x[:, c, :], bo_b, ALU.add)
            i.then_inc(xb_done, 1)

            def low_gate_up(e, slot):
                wait(pool, whg_done, e + 1)
                wait(pool, gu_done, (e - 1) * 4)
                g.tensor_tensor(WLg[slot][:, :, :, :].rearrange("p k g f -> p (k g f)"), raw_g[slot][:, :],
                                WHg[slot][:, :, :, :].rearrange("p k g f -> p (k g f)").bitcast(F32), ALU.subtract
                                ).then_inc(wlg_done, 1)

            def low_down(e, slot):
                wait(pool, whd_done, e + 1)
                wait(pool, y_done, (e - 1) * 2)
                g.tensor_tensor(WLd[slot][:, :, :].rearrange("p k d -> p (k d)"), raw_w[slot][:, :],
                                WHd[slot][:, :, :].rearrange("p k d -> p (k d)").bitcast(F32), ALU.subtract
                                ).then_inc(wld_done, 1)

            def low_keys(m):
                pool.wait_ge(kh_done, m + 1)
                g.tensor_tensor(kl[m], kpar[:, m, :, :], kh[m].bitcast(F32), ALU.subtract).then_inc(kl_done, 1)

            low_keys(0)
            low_keys(1)
            low_gate_up(0, 0)
            low_down(0, 0)
            low_gate_up(1, 1)
            for n in range(1, 5):
                rstds(n)

            def expert(e, slot, pair):
                for m in range(2):
                    pool.wait_ge(sig_done, e * 2 + (m + 1))
                    wait(pool, hid_done, e * 2 + (m - 1))
                    g.tensor_tensor(glu[:, m, :], gcl[:, m, :], sig[:, m, :], ALU.mult).then_inc(glu_done, 1)
                if not isinstance(e, int) or e + 2 < E:
                    low_gate_up(e + 2, slot)
                if not isinstance(e, int) or e + 1 < E:
                    low_down(e + 1, 1 - slot)

            def last():
                for n, (b, m) in enumerate(PARTS):
                    half_ = slice(b * S, (b + 1) * S)
                    pool.wait_ge(sig_done, LAST * KD + n + 1)
                    pool.wait_ge(hid_done, LAST * KD)
                    g.tensor_tensor(glu[:, m, half_], gcl[:, m, half_], sig[:, m, half_], ALU.mult).then_inc(glu_done, 1)
                for c in range(NC):
                    pool.wait_ge(scaled_done, c + 1)
                    pool.wait_ge(acc_done, (LAST - 1) * NC + c + 1)
                    g.tensor_tensor(acc[:, c, :], acc[:, c, :], xn[:, c, :], ALU.add).then_inc(added_done, 1)

            all_experts(pool, expert, last)

        @block.scalar
        def _(act):
            a = nc.scalar
            for c in (1, 3):
                act.dma_start(x[:, c, :], xv[:, c, :]).then_inc(x_in[c], 16)
            act.dma_start(rows[:, :], rows_d.rearrange("(a n) -> a n", a=1).to_broadcast([P, 2 * D + E])).then_inc(row_in, 16)
            act.dma_start(params[:, :], params_d).then_inc(param_in, 16)
            act.dma_start(mask8[:, :], mask_d.rearrange("(a n) -> a n", a=1)).then_inc(mask_in, 16)
            act.dma_start(dbias[:, :], dbias_d).then_inc(dbias_in, 16)
            a.preload_act_table_set("natural_log_exp_and_others")

            act.wait_ge(lnT_done, 1)
            a.activation(xT[:, :, 0:S], PS[:, 0, :].rearrange("p (k n) -> p k n", k=KD), ACT.Copy).then_inc(xT_done[0], 1)

            def high_gate_up(e, slot, pair):
                act.wait_ge(raw_g_in[slot], pair * 16 + 16)
                wait(act, gu_done, (e - 1) * 4)
                a.activation(WHg[slot][:, :, :, :].rearrange("p k g f -> p (k g f)"), raw_g[slot][:, :], ACT.Copy
                             ).then_inc(whg_done, 1)

            def high_down(e, slot, pair):
                act.wait_ge(raw_w_in[slot], pair * 16 + 16)
                wait(act, y_done, (e - 1) * 2)
                a.activation(WHd[slot][:, :, :].rearrange("p k d -> p (k d)"), raw_w[slot][:, :], ACT.Copy
                             ).then_inc(whd_done, 1)

            high_gate_up(0, 0, 0)
            for m in range(KD):
                act.wait_ge(k_done, m + 1)
                a.activation(kh[m], kpar[:, m, :, :], ACT.Copy).then_inc(kh_done, 1)
            for m in range(KD):
                act.wait_ge(q_done, m + 1)
                a.activation(qh[m], q2[m], ACT.Copy).then_inc(qh_done, 1)

            def exps(v):
                for j in range(2):
                    act.wait_ge(max_done, 2 * v + j + 1)
                    if v >= 2:
                        act.wait_ge(pT_done, 2 * v + j - 3)
                    for qc, cols in ((0, slice(0, P)), (1, slice(P, BLK * P))):
                        i = a.activation(pr[:, v % 2, j, cols], PS[:, 2 * (v % 3) + j, cols], ACT.Exp,
                                         bias=nmax[:, v % 2, j, qc:qc + 1])
                    i.then_inc(exp_done, 1)

            def context_exp(c):
                act.wait_ge(xbias_done, c + 1)
                if c >= 2:
                    act.wait_ge(xpT_done, c - 1)
                a.activation(xp[c % 2], PS[:, XS_BANK[c], :], ACT.Exp, bias=xbias[:, c:c + 1], scale=xscale[:, c:c + 1],
                             accum_out=xsum[:, c:c + 1]).then_inc(xexp_done, 1)

            def context_take(c):
                act.wait_ge(xpT_done, c + 1)
                if c >= 2:
                    act.wait_ge(xav_done, c - 1)
                a.activation(xpt[c % 2].rearrange("p h q -> p (h q)"), PS[:, XT_BANK[c], :], ACT.Copy
                             ).then_inc(xpt_done, 1)

            for v in range(NV + 2):
                if v < NV:
                    exps(v)
                if 1 <= v <= NV:
                    w = v - 1
                    act.wait_ge(pT_done, 2 * w + 2)
                    if w >= 4:
                        act.wait_ge(av_done, w // 2 - 1)
                    a.activation(pt[:, w // 2 % 2, 2 * (w % 2) + 1, :, :].rearrange("p c q -> p (c q)"),
                                 PS[:, 2 * (w % 3) + 1, 0:BLK * P], ACT.Copy).then_inc(pt_done[1], 1)
                if v >= 3 and v % 2 == 1:
                    u = (v - 3) // 2
                    b, hg = divmod(u, NG)
                    act.wait_ge(av_done, u + 1)
                    a.activation(osum[:, hg, b * S:(b + 1) * S], PS[:, 6, 0:S], ACT.Copy).then_inc(o_done, 1)
                if v == NV:
                    context_exp(0)
                if v == 4:
                    high_down(0, 0, 0)
                if v == 5:
                    high_gate_up(1, 1, 0)
            context_take(0)
            context_exp(1)

            def take_turned(dst, b, bank, n, done):
                act.wait_ge(lnT_done, n)
                a.activation(dst[:, :, b * S:(b + 1) * S], PS[:, bank, :].rearrange("p (k n) -> p k n", k=KD), ACT.Copy
                             ).then_inc(done, 1)

            def take_chunk(dst, c, bank, n, done):
                act.wait_ge(lnT_done, n)
                a.activation(dst[:, :, c * P:(c + 1) * P], PS[:, bank, 0:KD * P].rearrange("p (k n) -> p k n", k=KD), ACT.Copy
                             ).then_inc(done, 1)

            def high_x(b, count, tokens):
                act.wait_ge(xT_done[b], count)
                a.activation(XH[:, :, tokens], xT[:, :, tokens], ACT.Copy).then_inc(xh_done, 1)

            take_chunk(attT, 2, 7, 5, attT_done[1])
            context_take(1)
            take_chunk(attT, 3, 3, 6, attT_done[1])
            take_chunk(xT, 2, 7, 7, xT_done[1])
            take_chunk(xT, 3, 3, 8, xT_done[1])
            context_exp(2)
            take_turned(xT, 0, 0, 9, xT_done[0])
            context_exp(3)
            context_take(2)
            high_x(0, 3, slice(0, S))
            context_take(3)
            take_chunk(xT, 2, 6, 10, xT_done[1])
            high_x(1, 4, slice(S, S + P))
            take_chunk(xT, 3, 4, 11, xT_done[1])
            high_x(1, 5, slice(S + P, T))
            act.wait_ge(dlog_done, 1)
            a.activation(elog[:, :, :], dlog[:, :, :], ACT.Exp).then_inc(elog_done, 1)

            def expert(e, slot, pair):
                for m in range(2):
                    act.wait_ge(gcl_done, e * 2 + (m + 1))
                    wait(act, glu_done, e * 2 + (m - 1))
                    a.activation(sig[:, m, :], gcl[:, m, :], ACT.Sigmoid, scale=ALPHA).then_inc(sig_done, 1)

                def high(m):
                    act.wait_ge(hid_done, e * 2 + (m + 1))
                    wait(act, y_done, (e - 1) * 2)
                    a.activation(HH[slot][:, m, :], hid[:, m, :], ACT.Copy).then_inc(hh_done, 1)

                high(0)
                if not isinstance(e, int) or e + 2 < E:
                    high_gate_up(e + 2, slot, pair + 1)
                high(1)
                if not isinstance(e, int) or e + 1 < E:
                    high_down(e + 1, 1 - slot, pair + slot)

            def scale_outputs(b):
                act.wait_ge(y_done, (LAST - 1) * 2 + b + 1)
                for c in range(b * QC, (b + 1) * QC):
                    a.activation(xn[:, c, :], PS[:, 4 + c // 2, (c % 2) * D:(c % 2 + 1) * D], ACT.Copy,
                                 scale=score[:, c, LAST - 1:LAST]).then_inc(scaled_done, 1)

            def last():
                def sigmoid(b, m):
                    half_ = slice(b * S, (b + 1) * S)
                    act.wait_ge(gcl_done, LAST * KD + b * KD + m + 1)
                    act.wait_ge(glu_done, LAST * KD)
                    a.activation(sig[:, m, half_], gcl[:, m, half_], ACT.Sigmoid, scale=ALPHA).then_inc(sig_done, 1)

                def high(b, m):
                    half_ = slice(b * S, (b + 1) * S)
                    act.wait_ge(hid_done, LAST * KD + b * KD + m + 1)
                    act.wait_ge(y_done, (LAST - 1) * 2)
                    a.activation(HH[1][:, m, half_], hid[:, m, half_], ACT.Copy).then_inc(hh_done, 1)

                sigmoid(0, 0)
                sigmoid(0, 1)
                high(0, 0)
                sigmoid(1, 0)
                high(0, 1)
                sigmoid(1, 1)
                scale_outputs(0)
                high(1, 0)
                high(1, 1)
                scale_outputs(1)

            all_experts(act, expert, last)

        @block.vector
        def _(dve):
            v_ = nc.vector
            step = [0]

            def link(ins):
                step[0] += 1
                ins.then_inc(dve_step, 1)
                dve.wait_ge(dve_step, step[0])

            def row_stats(src, c):
                v_.bn_stats(stats[:, c, :], src[:, c, :]).then_inc(bn_done, 1)

            def variances(n, chunks):
                dve.wait_ge(bn_done, NC if n == 0 else NC + n * QC)
                for c in chunks:
                    i = v_.bn_aggr(mv[:, c, :], stats[:, c, :])
                link(i)
                cs = slice(chunks[0], chunks[-1] + 1)
                v_.tensor_scalar(ve[:, cs], mv[:, cs, 1], EPS, None, ALU.add).then_inc(stat_done, 1)

            def normalise(src, n, chunks):
                dve.wait_ge(rstd_done, n + 1)
                for c in chunks:
                    v_.tensor_scalar(xn[:, c, :], src[:, c, :], mv[:, c, 0:1], rstd[:, c:c + 1], ALU.subtract, ALU.mult
                                     ).then_inc(xn_done, 1)

            for c in range(NC):
                dve.wait_ge(x_in[c], 16)
                row_stats(x, c)
            variances(0, range(NC))
            normalise(x, 0, range(NC))
            dve.wait_ge(lnT_done, 2)
            v_.tensor_copy(xT[:, :, S:T], PS[:, 1, :].rearrange("p (k n) -> p k n", k=KD)).then_inc(xT_done[1], 1)

            def take_keys(m):
                dve.wait_ge(k_ps, m + 1)
                for r in range(2):
                    i = v_.tensor_scalar(kpar[:, m, r, :], PS[:, 4 + m, :], bk[:, m:m + 1], parity[:, r:r + 1], ALU.add, ALU.mult)
                i.then_inc(k_done, 1)

            def take_queries(m):
                dve.wait_ge(q_ps, m + 1)
                v_.tensor_scalar(qT[:, m, :], PS[:, 2 + m, :], bq[:, m:m + 1], DH ** -0.25, ALU.add, ALU.mult
                                 ).then_inc(q_done, 1)

            dve.wait_ge(mask_done, 1)
            v_.tensor_reduce(parity[:, :], headmask[:, :].rearrange("p (i r) -> p r i", r=2), AX.X, ALU.add).then_inc(parity_done, 1)
            dve.wait_ge(parity_done, 1)
            dve.wait_ge(param_in, 16)
            v_.tensor_scalar(bup1[:, :, :], gub[:, :, 1, :], 1.0, None, ALU.add)
            dve.wait_ge(mask_in, 16)
            link(v_.tensor_copy(maskf[:, :], mask8[:, :]))
            take_keys(0)
            v_.tensor_scalar(pen[:, :], maskf[:, :], -1.0, -NEG, ALU.add, ALU.mult).then_inc(pen_done, 1)
            take_keys(1)
            v_.tensor_reduce(valid1[:, :], maskf[:, :].rearrange("p (b m) -> p b m", b=B), AX.X, ALU.max).then_inc(pen_done, 1)
            take_queries(0)
            take_queries(1)
            for m in range(KD):
                dve.wait_ge(qh_done, m + 1)
                v_.tensor_tensor(ql[m], q2[m], qh[m].bitcast(F32), ALU.subtract).then_inc(ql_done, 1)
            dve.wait_ge(row_in, 16)

            def take_values(b):
                for c in range(b * QC, (b + 1) * QC):
                    dve.wait_ge(v_ps, c // 2 * 2 + 2)
                    v_.tensor_tensor(vp[:, c, :, 0:DH], PS[:, 6 + c // 2, (c % 2) * D:(c % 2 + 1) * D].rearrange("p (h d) -> p h d", d=DH),
                                     bv_b.rearrange("p (h d) -> p h d", d=DH), ALU.add).then_inc(v_done, 1)

            take_values(0)

            def outputs(b, qc, bank):
                dve.wait_ge(back_done, b * QC + qc + 1)
                heads = PS[:, bank, :].rearrange("p (h i) -> p h i", i=HP)
                link(v_.reciprocal(rsum[:, qc, :], heads[:, :, DH]))
                v_.tensor_tensor(att[:, b * QC + qc, :].rearrange("p (h i) -> p h i", i=DH), heads[:, :, 0:DH],
                                 rsum[:, qc, :].unsqueeze(2).to_broadcast([P, H, DH]), ALU.mult).then_inc(att_done, 1)

            def residual(b, j, place):
                dve.wait_ge(proj_done, b * QC + j + 1)
                link(v_.tensor_tensor(x2[:, b * QC + j, :], place, xb[:, b * QC + j, :], ALU.add))
                row_stats(x2, b * QC + j)

            def centre(b):
                cs = slice(b * QC, (b + 1) * QC)
                dve.wait_ge(bn_done, NC + (b + 1) * QC)
                for c in range(b * QC, (b + 1) * QC):
                    i = v_.bn_aggr(mv[:, c, :], stats[:, c, :])
                link(i)
                v_.tensor_scalar(ve[:, cs], mv[:, cs, 1], EPS, None, ALU.add).then_inc(stat_done, 1)
                for c in range(b * QC, (b + 1) * QC):
                    v_.tensor_scalar(xn[:, c, :], x2[:, c, :], mv[:, c, 0:1], None, ALU.subtract).then_inc(xn_done, 1)

            def context_scale(b):
                cs = slice(b * QC, (b + 1) * QC)
                dve.wait_ge(rstd_done, b + 2)
                link(v_.tensor_scalar(xscale[:, cs], rstd[:, cs], D ** -0.5, None, ALU.mult))

            def context_max(c):
                dve.wait_ge(xs_done, c + 1)
                link(v_.tensor_reduce(xmax[:, c:c + 1], PS[:, XS_BANK[c], :], AX.X, ALU.max))
                v_.tensor_scalar(xbias[:, c:c + 1], xmax[:, c:c + 1], -1.0, xscale[:, c:c + 1], ALU.mult, ALU.mult
                                 ).then_inc(xbias_done, 1)

            def context_weight(c):
                dve.wait_ge(xexp_done, c + 1)
                link(v_.reciprocal(xrec[:, c:c + 1], xsum[:, c:c + 1]))
                link(v_.tensor_tensor(xrv[:, c:c + 1], xrec[:, c:c + 1], valid[:, c // QC:c // QC + 1], ALU.mult))

            def context_out(c):
                dve.wait_ge(xav_done, c + 1)
                v_.scalar_tensor_tensor(out=x3[:, c, :], in0=PS[:, XV_BANK[c], 0:D], scalar=xrv[:, c:c + 1],
                                        in1=x2[:, c, :], op0=ALU.mult, op1=ALU.add).then_inc(x3_done, 1)

            def context_stats(c):
                dve.wait_ge(x3_done, c + 1)
                row_stats(x3, c)

            for v in range(NV + 2):
                if v < NV:
                    for j in range(2):
                        dve.wait_ge(sc_done, 2 * v + j + 1)
                        if v >= 2:
                            dve.wait_ge(exp_done, 2 * v + j - 3)
                        for qc, cols in ((0, slice(0, P)), (1, slice(P, BLK * P))):
                            i = v_.tensor_reduce(nmax[:, v % 2, j, qc:qc + 1], PS[:, 2 * (v % 3) + j, cols], AX.X, ALU.max, negate=True)
                        i.then_inc(max_done, 1)
                if v == NV:
                    dve.wait_ge(lnT_done, 4)
                    v_.tensor_copy(xT[:, :, 0:S], PS[:, 7, :].rearrange("p (k n) -> p k n", k=KD)).then_inc(xT_done[0], 1)
                if v == 1:
                    take_values(1)
                if v == TAIL + 4:
                    context_scale(0)
                if 1 <= v <= NV:
                    w = v - 1
                    dve.wait_ge(pT_done, 2 * w + 1)
                    if w >= 4:
                        dve.wait_ge(av_done, w // 2 - 1)
                    v_.tensor_copy(pt[:, w // 2 % 2, 2 * (w % 2), :, :].rearrange("p c q -> p (c q)"),
                                   PS[:, 2 * (w % 3), 0:BLK * P]).then_inc(pt_done[0], 1)
                if v == TAIL - 3:
                    dve.wait_ge(valid_ps, 1)
                    v_.tensor_copy(valid[:, :], PS[:, 7, 0:B]).then_inc(valid_done, 1)
                if v in (TAIL - 1, TAIL):
                    outputs(0, v - TAIL + 1, 7)
                if v == TAIL + 1:
                    dve.wait_ge(lnT_done, 3)
                    v_.tensor_copy(attT[:, :, 0:S], PS[:, 7, :].rearrange("p (k n) -> p k n", k=KD)).then_inc(attT_done[0], 1)
                if v == TAIL + 2:
                    dve.wait_ge(xb_done, 1)
                    dve.wait_ge(proj_done, QC)
                    residual(0, 0, PS[:, 7, 0:D])
                if v == TAIL + 3:
                    residual(0, 1, PS[:, 7, D:2 * D])
                    centre(0)
                if v >= NV:
                    context_max(v - NV)
            for qc in range(QC):
                outputs(1, qc, (5, 0)[qc])
            dve.wait_ge(valid_done, 1)
            context_weight(0)
            context_weight(1)
            context_out(0)
            for j in range(QC):
                residual(1, j, PS[:, (6, 5)[j], 0:D])
            centre(1)
            context_scale(1)
            context_out(1)
            context_stats(0)
            context_stats(1)
            variances(3, (0, 1))
            normalise(x3, 3, (0, 1))
            context_max(2)
            context_max(3)
            context_weight(2)
            context_weight(3)

            def low_x(n, tokens):
                dve.wait_ge(xh_done, n)
                v_.tensor_tensor(XL[:, :, tokens], xT[:, :, tokens], XH[:, :, tokens].bitcast(F32), ALU.subtract).then_inc(xl_done, 1)

            low_x(1, slice(0, S))
            context_out(2)
            context_stats(2)
            context_out(3)
            context_stats(3)
            variances(4, (2, 3))
            normalise(x3, 4, (2, 3))
            low_x(2, slice(S, S + P))
            low_x(3, slice(S + P, T))

            def clamp_gate(e, m):
                dve.wait_ge(gu_done, e * 4 + (2 * m + 1))
                wait(dve, glu_done, e * 2 + (m - 1))
                v_.tensor_scalar(gcl[:, m, :], PS[:, 2 * m, :], gub[:, bass.ds(e, 1), 0, m], LIMIT, ALU.add, ALU.min
                                 ).then_inc(gcl_done, 1)

            def clamp_up(e, m):
                dve.wait_ge(gu_done, e * 4 + (2 * m + 2))
                wait(dve, hid_done, e * 2 + (m - 1))
                v_.tensor_scalar(upc[:, m, :], PS[:, 2 * m + 1, :], bup1[:, bass.ds(e, 1), m], 1.0 - LIMIT, ALU.add, ALU.max
                                 ).then_inc(upc_done, 1)

            dve.wait_ge(logit_ps, 3)
            link(v_.tensor_tensor(logits[:, :, :], PS[:, 7, 0:NC * E].rearrange("p (c e) -> p c e", e=E),
                                  rb_b.unsqueeze(1).to_broadcast([P, NC, E]), ALU.add))
            for c in range(NC):
                i = v_.max(top8[:, c, :], logits[:, c, :])
            link(i)
            kth = top8[:, :, TOP_K - 1:TOP_K].to_broadcast([P, NC, E])
            v_.tensor_tensor(dlog[:, :, :], logits[:, :, :], top8[:, :, 0:1].to_broadcast([P, NC, E]), ALU.subtract
                             ).then_inc(dlog_done, 1)
            v_.tensor_tensor(gt[:, :, :], logits[:, :, :], kth, ALU.is_gt)
            link(v_.tensor_tensor(eq[:, :, :], logits[:, :, :], kth, ALU.is_equal))
            clamp_gate(0, 0)
            link(v_.tensor_reduce(cnt[:, :], gt[:, :, :], AX.X, ALU.add))
            v_.tensor_scalar(need[:, :], cnt[:, :], -1.0, float(TOP_K), ALU.mult, ALU.add)
            for c in range(NC):
                i = v_.tensor_tensor_scan(rank[:, c, :], ones_f[:, :], eq[:, c, :], 0.0, ALU.mult, ALU.add)
            link(i)
            clamp_up(0, 0)
            link(v_.tensor_tensor(within[:, :, :], rank[:, :, :], need[:, :].unsqueeze(2).to_broadcast([P, NC, E]), ALU.is_le))
            link(v_.tensor_tensor(sel_eq[:, :, :], eq[:, :, :], within[:, :, :], ALU.mult))
            link(v_.tensor_tensor(sel[:, :, :], sel_eq[:, :, :], gt[:, :, :], ALU.add))
            dve.wait_ge(elog_done, 1)
            link(v_.tensor_tensor(esel[:, :, :], elog[:, :, :], sel[:, :, :], ALU.mult))
            link(v_.tensor_reduce(etot[:, :], esel[:, :, :], AX.X, ALU.add))
            link(v_.reciprocal(erec[:, :], etot[:, :]))
            v_.tensor_tensor(score[:, :, :], esel[:, :, :], erec[:, :].unsqueeze(2).to_broadcast([P, NC, E]), ALU.mult
                             ).then_inc(score_done, 1)

            def weighted_sum(e, slot, chunks):
                for c in chunks:
                    if c % 2 == 0:
                        dve.wait_ge(y_done, e * 2 + (c // 2 + 1))
                    dve.wait_ge(acc_done, e * NC + (c + 1))
                    v_.scalar_tensor_tensor(out=acc[:, c, :], in0=PS[:, 4 + 2 * slot + c // 2, (c % 2) * D:(c % 2 + 1) * D],
                                            scalar=score[:, c, bass.ds(e, 1)], in1=acc[:, c, :], op0=ALU.mult, op1=ALU.add
                                            ).then_inc(acc_done, 1)

            def expert(e, slot, pair):
                def product(m):
                    dve.wait_ge(glu_done, e * 2 + (m + 1))
                    dve.wait_ge(upc_done, e * 2 + (m + 1))
                    wait(dve, hl_done, e * 2 + (m - 1))
                    v_.scalar_tensor_tensor(out=hid[:, m, :], in0=upc[:, m, :], scalar=1.0 + LIMIT, in1=glu[:, m, :],
                                            op0=ALU.min, op1=ALU.mult).then_inc(hid_done, 1)

                def low(m):
                    dve.wait_ge(hh_done, e * 2 + (m + 1))
                    v_.tensor_tensor(HL[slot][:, m, :], hid[:, m, :], HH[slot][:, m, :].bitcast(F32), ALU.subtract
                                     ).then_inc(hl_done, 1)

                if not isinstance(e, int) or e > 0:
                    clamp_gate(e, 0)
                    clamp_up(e, 0)
                clamp_gate(e, 1)
                product(0)
                clamp_up(e, 1)
                if isinstance(e, int) and e == 0:
                    dve.wait_ge(scoreT_ps, 1)
                    v_.tensor_copy(scoreT[:, :], PS[0:E, 5, :]).then_inc(scoreT_done, 1)
                low(0)
                product(1)
                if isinstance(e, int) and e == 0:
                    low(1)
                    for c in range(NC):
                        dve.wait_ge(dbias_ps, c // 2 * 2 + 2)
                        v_.tensor_tensor(acc[:, c, :], PS[:, 6 + c // 2, (c % 2) * D:(c % 2 + 1) * D], x3[:, c, :], ALU.add
                                         ).then_inc(acc_done, 1)
                else:
                    weighted_sum(e - 1, 1 - slot, (0, 1))
                    low(1)
                    if not isinstance(e, int) or e < LAST - 1:
                        weighted_sum(e - 1, 1 - slot, (2, 3))

            def last():
                first = LAST * KD + 1

                def clamps(b, m):
                    half_ = slice(b * S, (b + 1) * S)
                    dve.wait_ge(gu_done, LAST * 4 + 2 * m + 1)
                    dve.wait_ge(glu_done, LAST * KD)
                    v_.tensor_scalar(gcl[:, m, half_], PS[:, 2 * m, half_], gub[:, LAST, 0, m:m + 1], LIMIT, ALU.add, ALU.min
                                     ).then_inc(gcl_done, 1)
                    dve.wait_ge(gu_done, LAST * 4 + 2 * m + 2)
                    dve.wait_ge(hid_done, LAST * KD)
                    v_.tensor_scalar(upc[:, m, half_], PS[:, 2 * m + 1, half_], bup1[:, LAST, m:m + 1], 1.0 - LIMIT, ALU.add, ALU.max
                                     ).then_inc(upc_done, 1)

                def product(b, m):
                    half_, n = slice(b * S, (b + 1) * S), b * KD + m
                    dve.wait_ge(glu_done, first + n)
                    dve.wait_ge(upc_done, first + n)
                    dve.wait_ge(hl_done, LAST * KD)
                    v_.scalar_tensor_tensor(out=hid[:, m, half_], in0=upc[:, m, half_], scalar=1.0 + LIMIT, in1=glu[:, m, half_],
                                            op0=ALU.min, op1=ALU.mult).then_inc(hid_done, 1)

                def low(b, m):
                    half_ = slice(b * S, (b + 1) * S)
                    dve.wait_ge(hh_done, first + b * KD + m)
                    v_.tensor_tensor(HL[1][:, m, half_], hid[:, m, half_], HH[1][:, m, half_].bitcast(F32), ALU.subtract
                                     ).then_inc(hl_done, 1)

                clamps(0, 0)
                clamps(0, 1)
                product(0, 0)
                clamps(1, 0)
                product(0, 1)
                clamps(1, 1)
                low(0, 0)
                low(0, 1)
                weighted_sum(LAST - 2, 1, (2, 3))
                product(1, 0)
                product(1, 1)
                low(1, 0)
                low(1, 1)
                for c in range(NC):
                    dve.wait_ge(y_done, LAST * 2 + max(c, 1))
                    dve.wait_ge(added_done, c + 1)
                    v_.scalar_tensor_tensor(out=acc[:, c, :], in0=PS[:, LAST_BANK[c], (c % 2) * D:(c % 2 + 1) * D],
                                            scalar=score[:, c, LAST:E], in1=acc[:, c, :], op0=ALU.mult, op1=ALU.add
                                            ).then_inc(acc_done, 1)

            all_experts(dve, expert, last)

        @block.tensor
        def _(pe):
            t = nc.tensor

            def transposes(src, b, bank, ready, count):
                for j in range(QC):
                    pe.wait_ge(ready, count - QC + j + 1)
                    for k in range(KD):
                        i = t.transpose(PS[:, bank, (k * 2 + j) * P:(k * 2 + j + 1) * P],
                                        src[:, b * QC + j, k * P:(k + 1) * P], ident[:, :])
                i.then_inc(lnT_done, 1)

            def turn_chunk(src, c, bank):
                for k in range(KD):
                    i = t.transpose(PS[:, bank, k * P:(k + 1) * P], src[:, c, k * P:(k + 1) * P], ident[:, :])
                i.then_inc(lnT_done, 1)

            pe.wait_ge(warm_done, 1)

            def keep_warm(bank, n):
                for _ in range(n):
                    t.matmul(PS[:, bank, :], warm[:, 0:P], warm[:, :], start=True, stop=True)

            keep_warm(7, 14)
            pe.wait_ge(ident_done, 1)
            for b in range(B):
                transposes(xn, b, b, xn_done, (b + 1) * QC)
            for j, bank, done in ((1, 4, k_ps), (0, 2, q_ps)):
                pe.wait_ge(qkv_in[j], 16)
                for m in range(KD):
                    for b in range(B):
                        pe.wait_ge(xT_done[b], 1)
                        for k in range(KD):
                            i = t.matmul(PS[:, bank + m, b * S:(b + 1) * S], wqkv[:, j, k, m * P:(m + 1) * P], xT[:, k, b * S:(b + 1) * S],
                                         start=(k == 0), stop=(k == KD - 1))
                    i.then_inc(done, 1)

            def project_values(b):
                for c in range(b * QC, (b + 1) * QC):
                    for k in range(KD):
                        i = t.matmul(PS[:, 6 + c // 2, (c % 2) * D:(c % 2 + 1) * D], xT[:, k, c * P:(c + 1) * P], wqkv[:, 2, k, :],
                                     start=(k == 0), stop=(k == KD - 1))
                    i.then_inc(v_ps, 1)

            pe.wait_ge(qkv_in[2], 16)
            project_values(0)

            pe.wait_ge(q_done, KD)

            def scores(v):
                u, pair = divmod(v, 2)
                b, hg = divmod(u, NG)
                g, r = divmod(hg, 2)
                if v in (0, 4):
                    pe.wait_ge(kl_done, g + 1)
                    pe.wait_ge(ql_done, g + 1)
                if v >= 3:
                    for j in range(2):
                        pe.wait_ge(pt_done[j], v - 2)
                for j in range(2):
                    diagonal = PS[:, 2 * (v % 3) + j, :].rearrange("p (a k) -> p a k", a=2)[:, :, 0:P]
                    t.matmul(diagonal, ident_bf[:, :], causal[:, :].unsqueeze(1).to_broadcast([P, 2, P]), start=True, stop=False,
                             skip_group_check=True)
                for j in range(2):
                    out, tile = PS[:, 2 * (v % 3) + j, :], slice(HP * (2 * pair + j), HP * (2 * pair + j + 1))
                    t.matmul(out[:, 0:P], qT[tile, g, b * S:b * S + P], kpar[tile, g, r, b * S:b * S + P],
                             start=False, stop=True, skip_group_check=True)
                    for q, k in ((qh, kh), (ql, kh), (qh, kl)):
                        i = t.matmul(out[:, P:BLK * P], q[g][tile, b, :], k[g][tile, r, b * S:(b + 1) * S],
                                     start=False, stop=True, skip_group_check=True)
                    i.then_inc(sc_done, 1)

            def turn(v):
                for j in range(2):
                    pe.wait_ge(exp_done, 2 * v + j + 1)
                    for n in range(BLK):
                        i = t.transpose(PS[:, 2 * (v % 3) + j, n * P:(n + 1) * P], pr[:, v % 2, j, n * P:(n + 1) * P], ident[:, :])
                    i.then_inc(pT_done, 1)

            def values(u):
                b, hg = divmod(u, NG)
                if u % NG == 0:
                    pe.wait_ge(v_done, QC * (b + 1))
                for j in range(2):
                    pe.wait_ge(pt_done[j], 2 * u + 2)
                if u >= 1:
                    pe.wait_ge(o_done, u)
                for n, (qc, kc) in enumerate(((0, 0), (1, 0), (1, 1))):
                    for h in range(HG):
                        i = t.matmul(PS[HP * h:HP * (h + 1), 6, qc * P:(qc + 1) * P], vp[:, b * QC + kc, hg * HG + h, :],
                                     pt[:, u % 2, h, n, :], start=(kc == 0), stop=(kc == qc))
                i.then_inc(av_done, 1)

            def turn_back(b, qc, bank):
                pe.wait_ge(o_done, (b + 1) * NG)
                for hg in range(NG):
                    i = t.transpose(PS[:, bank, hg * P:(hg + 1) * P], osum[:, hg, b * S + qc * P:b * S + (qc + 1) * P], ident[:, :])
                i.then_inc(back_done, 1)

            def project(b, places):
                for j in range(QC):
                    c = b * QC + j
                    pe.wait_ge(attT_done[b], 1 if b == 0 else j + 1)
                    for k in range(KD):
                        i = t.matmul(places[j], attT[:, k, c * P:(c + 1) * P], wo[:, k, :],
                                     start=(k == 0), stop=(k == KD - 1))
                    i.then_inc(proj_done, 1)

            def context_scores(c):
                b = c // QC
                pe.wait_ge(xT_done[b], 2 if b == 0 else c - QC + 2)
                for k in range(KD):
                    t.matmul(PS[:, XS_BANK[c], :], xT[:, k, c * P:(c + 1) * P], ctxT[:, b * KD + k, :], start=(k == 0), stop=False)
                t.matmul(PS[:, XS_BANK[c], :], ones_bf[:, :], pen[:, b * M:(b + 1) * M], start=False, stop=True
                         ).then_inc(xs_done, 1)

            def context_turn(c):
                pe.wait_ge(xexp_done, c + 1)
                for j in range(KM):
                    i = t.transpose(PS[:, XT_BANK[c], j * P:(j + 1) * P], xp[c % 2][:, j * P:(j + 1) * P], ident[:, :])
                i.then_inc(xpT_done, 1)

            def context_values(c):
                pe.wait_ge(xpt_done, c + 1)
                for j in range(KM):
                    i = t.matmul(PS[:, XV_BANK[c], 0:D], xpt[c % 2][:, j, :], ctx_sb[:, (c // QC) * KM + j, :],
                                 start=(j == 0), stop=(j == KM - 1))
                i.then_inc(xav_done, 1)

            def logits_of(b, count, chunks):
                pe.wait_ge(xT_done[b], count)
                for c in chunks:
                    for k in range(KD):
                        i = t.matmul(PS[:, 7, c * E:(c + 1) * E], xT[:, k, c * P:(c + 1) * P], routerT[:, k, :],
                                     start=(k == 0), stop=(k == KD - 1))
                i.then_inc(logit_ps, 1)

            for v in range(NV + 2):
                if v < NV:
                    scores(v)
                if v == 1:
                    project_values(1)
                if v == NV:
                    transposes(xn, 0, 7, xn_done, NC + QC)
                if 1 <= v <= NV:
                    turn(v - 1)
                if v >= 3 and v % 2 == 1:
                    values((v - 3) // 2)
                if v == TAIL - 3:
                    pe.wait_ge(pen_done, 2)
                    pe.wait_ge(v_done, NC)
                    t.matmul(PS[:, 7, 0:B], one1[:, :], valid1[:, :], start=True, stop=True).then_inc(valid_ps, 1)
                if v == TAIL - 1:
                    pe.wait_ge(valid_done, 1)
                    turn_back(0, 0, 7)
                if v == TAIL:
                    pe.wait_ge(att_done, 1)
                    turn_back(0, 1, 7)
                if v == TAIL + 1:
                    pe.wait_ge(att_done, QC)
                    transposes(att, 0, 7, att_done, QC)
                if v == TAIL + 2:
                    pe.wait_ge(wo_in, 16)
                    project(0, [PS[:, 7, j * D:(j + 1) * D] for j in range(QC)])
                if v == NV:
                    pe.wait_ge(ctxT_in, 16)
                    context_scores(0)
            context_scores(1)
            context_turn(0)
            for qc in range(QC):
                turn_back(1, qc, (5, 0)[qc])
            pe.wait_ge(ctx_in, 16)
            context_values(0)
            pe.wait_ge(att_done, NC)
            turn_chunk(att, 2, 7)
            context_turn(1)
            turn_chunk(att, 3, 3)
            project(1, [PS[:, 6, 0:D], PS[:, 5, 0:D]])
            context_values(1)
            keep_warm(0, 2)
            for j in range(QC):
                pe.wait_ge(xn_done, NC + QC + j + 1)
                turn_chunk(xn, QC + j, (7, 3)[j])
            keep_warm(0, 1)
            context_scores(2)
            context_scores(3)
            transposes(xn, 0, 0, xn_done, NC + 3 * QC)
            context_turn(2)
            logits_of(0, 3, (0, 1))
            context_turn(3)
            context_values(2)
            context_values(3)

            def first_gate_up(b):
                pe.wait_ge(wlg_done, 1)
                pe.wait_ge(xl_done, 1 if b == 0 else 3)
                for m in range(2):
                    for part in range(2):
                        n = 0
                        for k in range(KD):
                            for w, xx in ((WHg, XH), (WHg, XL), (WLg, XH)):
                                i = t.matmul(PS[:, 2 * m + part, b * S:(b + 1) * S], w[0][:, k, part, m * P:(m + 1) * P],
                                             xx[:, k, b * S:(b + 1) * S], start=(n == 0), stop=(n == 3 * KD - 1))
                                n += 1
                        if b == B - 1:
                            i.then_inc(gu_done, 1)

            first_gate_up(0)
            for j in range(QC):
                pe.wait_ge(xn_done, NC + 3 * QC + j + 1)
                turn_chunk(xn, QC + j, (6, 4)[j])
            keep_warm(5, 1)
            logits_of(1, 4, (2,))
            keep_warm(5, 1)
            logits_of(1, 5, (3,))
            keep_warm(5, 1)
            first_gate_up(1)

            def turn_scores():
                pe.wait_ge(score_done, 1)
                for c in range(NC):
                    i = t.transpose(PS[0:E, 5, c * P:(c + 1) * P], score[:, c, :], ident[:, :])
                i.then_inc(scoreT_ps, 1)

            def gate_up(e, slot):
                pe.wait_ge(wlg_done, e + 1)
                for m in range(2):
                    for part in range(2):
                        wait(pe, gcl_done if part == 0 else upc_done, e * 2 + (m - 1))
                        n = 0
                        for k in range(KD):
                            for w, xx in ((WHg, XH), (WHg, XL), (WLg, XH)):
                                i = t.matmul(PS[:, 2 * m + part, :], w[slot][:, k, part, m * P:(m + 1) * P], xx[:, k, :],
                                             start=(n == 0), stop=(n == 3 * KD - 1))
                                n += 1
                        i.then_inc(gu_done, 1)
                    if m == 0 and isinstance(e, int) and e == 1:
                        turn_scores()

            def down(e, slot):
                pe.wait_ge(hl_done, e * 2 + 2)
                pe.wait_ge(wld_done, e + 1)
                wait(pe, acc_done, e * NC)
                for c in range(NC):
                    n = 0
                    for k in range(KD):
                        for hh, w in ((HH, WHd), (HL, WHd), (HH, WLd)):
                            i = t.matmul(PS[:, 4 + 2 * slot + c // 2, (c % 2) * D:(c % 2 + 1) * D], hh[slot][:, k, c * P:(c + 1) * P],
                                         w[slot][:, k, :], start=(n == 0), stop=(n == 3 * KD - 1))
                            n += 1
                    if c % 2 == 1:
                        i.then_inc(y_done, 1)

            def weighted_biases():
                pe.wait_ge(scoreT_done, 1)
                pe.wait_ge(dbias_in, 16)
                for c in range(NC):
                    t.matmul(PS[:, 6 + c // 2, (c % 2) * D:(c % 2 + 1) * D], scoreT[:, c * P:(c + 1) * P], dbias[:, :], start=True, stop=True
                             ).then_inc(dbias_ps, 1)

            def both(e, slot, pair):
                if not isinstance(e, int) or e + 1 < E:
                    gate_up(e + 1, 1 - slot)
                if isinstance(e, int) and e == 0:
                    weighted_biases()
                down(e, slot)

            def last():
                pe.wait_ge(acc_done, LAST * NC - NC + QC)
                keep_warm(6, 8)
                pe.wait_ge(wld_done, LAST + 1)
                for c in range(NC):
                    if c % QC == 0:
                        pe.wait_ge(hl_done, LAST * KD + (c // QC + 1) * KD)
                    n = 0
                    for k in range(KD):
                        for hh, w in ((HH, WHd), (HL, WHd), (HH, WLd)):
                            i = t.matmul(PS[:, LAST_BANK[c], (c % 2) * D:(c % 2 + 1) * D], hh[1][:, k, c * P:(c + 1) * P],
                                         w[1][:, k, :], start=(n == 0), stop=(n == 3 * KD - 1))
                            n += 1
                    if c >= 1:
                        i.then_inc(y_done, 1)
                    if c == QC - 1:
                        pe.wait_ge(acc_done, LAST * NC)
                        keep_warm(7, 3)

            all_experts(pe, both, last)


def kernel(**inputs):
    import numpy as np
    import concourse.bacc as bacc
    from concourse.bass_utils import run_bass_kernel_spmd

    a = {n: np.ascontiguousarray(v) for n, v in inputs.items()}

    def rows_in(w):
        return w.reshape(-1, P, w.shape[-1]).transpose(1, 0, 2)

    heads = np.arange(H).reshape(KD, HG, 2).transpose(0, 2, 1).reshape(-1)
    order = (heads[:, None] * DH + np.arange(DH)).reshape(-1)
    wqkv = np.stack([rows_in(w.T) for w in (a["L0_attn_Wq"], a["L0_attn_Wk"], a["L0_attn_Wv"][order])], axis=1)
    wo = rows_in(a["L0_attn_Wo"].T[order])
    gub = a["L0_ffn_gate_up_proj_bias"].reshape(E, KD, P, 2).transpose(2, 0, 3, 1)
    params = np.concatenate([a["L0_attn_bq"].reshape(KD, P).T, a["L0_attn_bk"].reshape(KD, P).T, gub.reshape(P, -1),
                             rows_in(a["L0_ffn_router_weight"].T).reshape(P, -1)], axis=1)
    rows = np.concatenate([a["L0_attn_bv"][order], a["L0_attn_bo"], a["L0_ffn_router_bias"]])
    gup = a["L0_ffn_gate_up_proj"].reshape(E, KD, P, F, 2).transpose(0, 2, 1, 4, 3).reshape(E, P, GU)
    down = a["L0_ffn_down_proj"].reshape(E, KD, P, D).transpose(0, 2, 1, 3).reshape(E, P, DW)
    ctxT = a["ctx_2048"].transpose(2, 0, 1).reshape(KD, P, B, M).transpose(1, 2, 0, 3).reshape(P, B * KD, M)
    arrays = {
        "x_d": a["x"], "ctx_d": a["ctx_2048"], "ctxT_d": ctxT, "wqkv_d": wqkv, "wo_d": wo, "params_d": params,
        "rows_d": rows, "mask_d": a["mask_BxS2_bk0"].reshape(-1), "dbias_d": a["L0_ffn_down_proj_bias"],
        "we_d": np.concatenate([gup, down], axis=2),
    }
    arrays = {n: np.ascontiguousarray(v) for n, v in arrays.items()}
    nc = bacc.Bacc("TRN2", target_bir_lowering=False, num_devices=1)
    args = [nc.dram_tensor(n, v.shape, mybir.dt.from_np(v.dtype), kind="ExternalInput").ap() for n, v in arrays.items()]
    out = nc.dram_tensor("out_d", (B, S, D), F32, kind="ExternalOutput").ap()
    decoder_layer(nc, *args, out)
    got = run_bass_kernel_spmd(nc, [arrays], core_ids=[0])
    return got.results[0]["out_d"]
```
